# Optimizing a Trainium2 kernel written in Bass

```python
import numpy as np
import jax
import jax.numpy as jnp

def _softmax(x, axis=-1):
    return jax.nn.softmax(x, axis=axis)

def _gelu(x):
    return jax.nn.gelu(x, approximate=True)

def _silu(x):
    return jax.nn.silu(x)

def _sigmoid(x):
    return jax.nn.sigmoid(x)

def _layernorm(x, axis=-1, eps=1e-05):
    m = jnp.mean(x, axis=axis, keepdims=True)
    v = jnp.var(x, axis=axis, keepdims=True)
    return (x - m) / jnp.sqrt(v + eps)

def _scatter_add(tgt, idx, src, axis=0):
    return tgt.at[idx].add(src)

def _segment_sum(src, seg, n):
    return jax.ops.segment_sum(src, seg, n)
kernel_name = 'mk_sandwich_d1_jaxref_r4_623ace'

def setup_inputs(seed: int=0):
    np.random.seed(seed)
    _w = jnp.asarray

    def _L0_attn_setup():
        import jax, jax.numpy as jnp
        import numpy as np
        B, T, C = (8, 512, 256)
        NL, LID = (12, 1)
        H = 4 * C

        def _ln(x, g, b):
            m = x.mean(-1, keepdims=True)
            v = ((x - m) ** 2).mean(-1, keepdims=True)
            return (x - m) * jax.lax.rsqrt(v + 1e-05) * g + b

        def _shift(x):
            return jnp.pad(x, ((0, 0), (1, 0), (0, 0)))[:, :-1]

        def _wkv(time_decay, time_first, k, v):
            w = -jnp.exp(time_decay)
            kt = jnp.moveaxis(k, 1, 0)
            vt = jnp.moveaxis(v, 1, 0)
            Bb, Cc = (k.shape[0], k.shape[2])
            init = (jnp.zeros((Bb, Cc), k.dtype), jnp.zeros((Bb, Cc), k.dtype), jnp.full((Bb, Cc), -1e+38, k.dtype))

            def step(carry, kv_t):
                aa, bb, pp = carry
                kk, vv = kv_t
                ww = time_first + kk
                p = jnp.maximum(pp, ww)
                e1 = jnp.exp(pp - p)
                e2 = jnp.exp(ww - p)
                out = (e1 * aa + e2 * vv) / (e1 * bb + e2)
                ww2 = pp + w
                p2 = jnp.maximum(ww2, kk)
                e1b = jnp.exp(ww2 - p2)
                e2b = jnp.exp(kk - p2)
                return ((e1b * aa + e2b * vv, e1b * bb + e2b, p2), out)
            _, out = jax.lax.scan(step, init, (kt, vt))
            return jnp.moveaxis(out, 0, 1)
        key = jax.random.key(seed)
        ks = jax.random.split(key, 8)
        f = lambda i, shape: 0.02 * jax.random.normal(ks[i], shape, jnp.float32)
        r01 = LID / (NL - 1)
        r10 = 1.0 - LID / NL
        h = np.arange(C, dtype=np.float64)
        decay = (-5 + 8 * (h / (C - 1)) ** (0.7 + 1.3 * r01)).astype(np.float32)
        zig = np.array([(i + 1) % 3 - 1 for i in range(C)]) * 0.5
        tfirst = (np.ones(C) * np.log(0.3) + zig).astype(np.float32)
        xpos = h / C
        tmk = (xpos ** r10).astype(np.float32)
        tmv = (xpos ** r10 + 0.3 * r01).astype(np.float32)
        tmr = (xpos ** (0.5 * r10)).astype(np.float32)
        cm = (xpos ** r10).astype(np.float32)
        return dict(x=jax.random.normal(ks[0], (B, T, C), jnp.float32), ln1_g=jnp.ones(C, jnp.float32), ln1_b=jnp.zeros(C, jnp.float32), ln2_g=jnp.ones(C, jnp.float32), ln2_b=jnp.zeros(C, jnp.float32), time_decay=jnp.asarray(decay), time_first=jnp.asarray(tfirst), time_mix_k=jnp.asarray(tmk), time_mix_v=jnp.asarray(tmv), time_mix_r=jnp.asarray(tmr), att_Wk=f(1, (C, C)), att_Wv=f(2, (C, C)), att_Wr=f(3, (C, C)), att_Wo=f(4, (C, C)), cm_k=jnp.asarray(cm), cm_r=jnp.asarray(cm), ffn_Wk=f(5, (H, C)), ffn_Wr=f(6, (C, C)), ffn_Wv=f(7, (C, H)))
    _L0_attn_in = _L0_attn_setup()

    def _L0_ffn_setup():
        import jax, jax.numpy as jnp
        import numpy as np
        B, S, D, H, E, F, K = (2, 256, 256, 16, 8, 1024, 2)
        EPS = 1e-05

        def _layernorm(x, g, b):
            mu = jnp.mean(x, axis=-1, keepdims=True)
            var = jnp.mean(jnp.square(x - mu), axis=-1, keepdims=True)
            return (x - mu) * jax.lax.rsqrt(var + EPS) * g + b
        key = jax.random.key(seed)
        ks = jax.random.split(key, 12)
        w = lambda k, shape: jax.random.normal(k, shape, dtype=jnp.float32) * 0.02
        return {'x': jax.random.normal(ks[0], (B, S, D), dtype=jnp.float32), 'ln1_g': jnp.ones((D,), jnp.float32), 'ln1_b': jnp.zeros((D,), jnp.float32), 'ln2_g': jnp.ones((D,), jnp.float32), 'ln2_b': jnp.zeros((D,), jnp.float32), 'Wq': w(ks[1], (D, D)), 'Wk': w(ks[2], (D, D)), 'Wv': w(ks[3], (D, D)), 'Wo': w(ks[4], (D, D)), 'Wg': w(ks[5], (D, E)), 'W1': w(ks[6], (E, D, F)), 'b1': jnp.zeros((E, F), jnp.float32), 'W2': w(ks[7], (E, F, D)), 'b2': jnp.zeros((E, D), jnp.float32)}
    _L0_ffn_in = _L0_ffn_setup()
    _d = {'L0_attn_x': _L0_attn_in['x'], 'L0_attn_ln1_g': _L0_attn_in['ln1_g'], 'L0_attn_ln1_b': _L0_attn_in['ln1_b'], 'L0_attn_ln2_g': _L0_attn_in['ln2_g'], 'L0_attn_ln2_b': _L0_attn_in['ln2_b'], 'L0_attn_time_decay': _L0_attn_in['time_decay'], 'L0_attn_time_first': _L0_attn_in['time_first'], 'L0_attn_time_mix_k': _L0_attn_in['time_mix_k'], 'L0_attn_time_mix_v': _L0_attn_in['time_mix_v'], 'L0_attn_time_mix_r': _L0_attn_in['time_mix_r'], 'L0_attn_att_Wk': _L0_attn_in['att_Wk'], 'L0_attn_att_Wv': _L0_attn_in['att_Wv'], 'L0_attn_att_Wr': _L0_attn_in['att_Wr'], 'L0_attn_att_Wo': _L0_attn_in['att_Wo'], 'L0_attn_cm_k': _L0_attn_in['cm_k'], 'L0_attn_cm_r': _L0_attn_in['cm_r'], 'L0_attn_ffn_Wk': _L0_attn_in['ffn_Wk'], 'L0_attn_ffn_Wr': _L0_attn_in['ffn_Wr'], 'L0_attn_ffn_Wv': _L0_attn_in['ffn_Wv'], 'L0_ffn_ln1_g': _L0_ffn_in['ln1_g'], 'L0_ffn_ln1_b': _L0_ffn_in['ln1_b'], 'L0_ffn_ln2_g': _L0_ffn_in['ln2_g'], 'L0_ffn_ln2_b': _L0_ffn_in['ln2_b'], 'L0_ffn_Wq': _L0_ffn_in['Wq'], 'L0_ffn_Wk': _L0_ffn_in['Wk'], 'L0_ffn_Wv': _L0_ffn_in['Wv'], 'L0_ffn_Wo': _L0_ffn_in['Wo'], 'L0_ffn_Wg': _L0_ffn_in['Wg'], 'L0_ffn_W1': _L0_ffn_in['W1'], 'L0_ffn_b1': _L0_ffn_in['b1'], 'L0_ffn_W2': _L0_ffn_in['W2'], 'L0_ffn_b2': _L0_ffn_in['b2']}
    _x0 = _d['L0_attn_x']
    _d['L0_attn_x'] = jax.random.normal(jax.random.fold_in(jax.random.key(seed), 1), (2, 2048, 256), dtype=_x0.dtype)
    del _x0
    return _d

def reference(L0_attn_x, L0_attn_ln1_g, L0_attn_ln1_b, L0_attn_ln2_g, L0_attn_ln2_b, L0_attn_time_decay, L0_attn_time_first, L0_attn_time_mix_k, L0_attn_time_mix_v, L0_attn_time_mix_r, L0_attn_att_Wk, L0_attn_att_Wv, L0_attn_att_Wr, L0_attn_att_Wo, L0_attn_cm_k, L0_attn_cm_r, L0_attn_ffn_Wk, L0_attn_ffn_Wr, L0_attn_ffn_Wv, L0_ffn_ln1_g, L0_ffn_ln1_b, L0_ffn_ln2_g, L0_ffn_ln2_b, L0_ffn_Wq, L0_ffn_Wk, L0_ffn_Wv, L0_ffn_Wo, L0_ffn_Wg, L0_ffn_W1, L0_ffn_b1, L0_ffn_W2, L0_ffn_b2):

    def _L0_attn_ref(x, ln1_g, ln1_b, ln2_g, ln2_b, time_decay, time_first, time_mix_k, time_mix_v, time_mix_r, att_Wk, att_Wv, att_Wr, att_Wo, cm_k, cm_r, ffn_Wk, ffn_Wr, ffn_Wv):
        import jax, jax.numpy as jnp
        import numpy as np
        B, T, C = (8, 512, 256)
        NL, LID = (12, 1)
        H = 4 * C

        def _ln(x, g, b):
            m = x.mean(-1, keepdims=True)
            v = ((x - m) ** 2).mean(-1, keepdims=True)
            return (x - m) * jax.lax.rsqrt(v + 1e-05) * g + b

        def _shift(x):
            return jnp.pad(x, ((0, 0), (1, 0), (0, 0)))[:, :-1]

        def _wkv(time_decay, time_first, k, v):
            w = -jnp.exp(time_decay)
            kt = jnp.moveaxis(k, 1, 0)
            vt = jnp.moveaxis(v, 1, 0)
            Bb, Cc = (k.shape[0], k.shape[2])
            init = (jnp.zeros((Bb, Cc), k.dtype), jnp.zeros((Bb, Cc), k.dtype), jnp.full((Bb, Cc), -1e+38, k.dtype))

            def step(carry, kv_t):
                aa, bb, pp = carry
                kk, vv = kv_t
                ww = time_first + kk
                p = jnp.maximum(pp, ww)
                e1 = jnp.exp(pp - p)
                e2 = jnp.exp(ww - p)
                out = (e1 * aa + e2 * vv) / (e1 * bb + e2)
                ww2 = pp + w
                p2 = jnp.maximum(ww2, kk)
                e1b = jnp.exp(ww2 - p2)
                e2b = jnp.exp(kk - p2)
                return ((e1b * aa + e2b * vv, e1b * bb + e2b, p2), out)
            _, out = jax.lax.scan(step, init, (kt, vt))
            return jnp.moveaxis(out, 0, 1)
        xa = _ln(x, ln1_g, ln1_b)
        xx = _shift(xa)
        xk = xa * time_mix_k + xx * (1 - time_mix_k)
        xv = xa * time_mix_v + xx * (1 - time_mix_v)
        xr = xa * time_mix_r + xx * (1 - time_mix_r)
        k = jnp.einsum('btc,oc->bto', xk, att_Wk)
        v = jnp.einsum('btc,oc->bto', xv, att_Wv)
        r = jnp.einsum('btc,oc->bto', xr, att_Wr)
        rwkv = jax.nn.sigmoid(r) * _wkv(time_decay, time_first, k, v)
        x = x + jnp.einsum('bto,co->btc', rwkv, att_Wo)
        xc = _ln(x, ln2_g, ln2_b)
        xx2 = _shift(xc)
        xk2 = xc * cm_k + xx2 * (1 - cm_k)
        xr2 = xc * cm_r + xx2 * (1 - cm_r)
        kk = jnp.square(jax.nn.relu(jnp.einsum('btc,hc->bth', xk2, ffn_Wk)))
        kv = jnp.einsum('bth,ch->btc', kk, ffn_Wv)
        rkv = jax.nn.sigmoid(jnp.einsum('btc,oc->bto', xr2, ffn_Wr)) * kv
        return x + rkv

    def _L0_ffn_ref(x, ln1_g, ln1_b, ln2_g, ln2_b, Wq, Wk, Wv, Wo, Wg, W1, b1, W2, b2):
        import jax, jax.numpy as jnp
        import numpy as np
        B, S, D, H, E, F, K = (2, 256, 256, 16, 8, 1024, 2)
        EPS = 1e-05

        def _layernorm(x, g, b):
            mu = jnp.mean(x, axis=-1, keepdims=True)
            var = jnp.mean(jnp.square(x - mu), axis=-1, keepdims=True)
            return (x - mu) * jax.lax.rsqrt(var + EPS) * g + b
        Bb, Ss, Dd = x.shape
        Dh = Dd // H
        h = _layernorm(x, ln1_g, ln1_b)
        q = (h @ Wq).reshape(Bb, Ss, H, Dh)
        k = (h @ Wk).reshape(Bb, Ss, H, Dh)
        v = (h @ Wv).reshape(Bb, Ss, H, Dh)
        scores = jnp.einsum('bqhd,bkhd->bhqk', q, k) / jnp.sqrt(jnp.float32(Dh))
        attn = jax.nn.softmax(scores, axis=-1)
        ctx = jnp.einsum('bhqk,bkhd->bqhd', attn, v).reshape(Bb, Ss, Dd)
        x = x + ctx @ Wo
        m = _layernorm(x, ln2_g, ln2_b)
        xt = m.reshape(-1, Dd)
        T = xt.shape[0]
        probs = jax.nn.softmax(xt @ Wg, axis=-1)
        wts, idx = jax.lax.top_k(probs, K)
        wts = wts / jnp.sum(wts, axis=-1, keepdims=True)
        h1 = jax.nn.gelu(jnp.einsum('td,edf->etf', xt, W1) + b1[:, None, :])
        ye = jnp.einsum('etf,efd->etd', h1, W2) + b2[:, None, :]
        sel = ye[idx, jnp.arange(T)[:, None], :]
        moe_out = jnp.sum(wts[..., None] * sel, axis=1).reshape(Bb, Ss, Dd)
        return x + moe_out
    x = L0_attn_x
    x = x + _layernorm(_L0_attn_ref(_layernorm(x, axis=-1), L0_attn_ln1_g, L0_attn_ln1_b, L0_attn_ln2_g, L0_attn_ln2_b, L0_attn_time_decay, L0_attn_time_first, L0_attn_time_mix_k, L0_attn_time_mix_v, L0_attn_time_mix_r, L0_attn_att_Wk, L0_attn_att_Wv, L0_attn_att_Wr, L0_attn_att_Wo, L0_attn_cm_k, L0_attn_cm_r, L0_attn_ffn_Wk, L0_attn_ffn_Wr, L0_attn_ffn_Wv), axis=-1)
    x = x + _layernorm(_L0_ffn_ref(_layernorm(x, axis=-1), L0_ffn_ln1_g, L0_ffn_ln1_b, L0_ffn_ln2_g, L0_ffn_ln2_b, L0_ffn_Wq, L0_ffn_Wk, L0_ffn_Wv, L0_ffn_Wo, L0_ffn_Wg, L0_ffn_W1, L0_ffn_b1, L0_ffn_W2, L0_ffn_b2), axis=-1)
    return x

_drawn_inputs = setup_inputs


def setup_inputs(seed=0):
    import zlib

    import numpy as np

    out = dict(_drawn_inputs(seed))
    spreads = {'L0_attn_ln1_g': (1.0, 0.6),
     'L0_attn_ln1_b': (0.0, 0.8),
     'L0_attn_ln2_g': (1.0, 0.6),
     'L0_attn_ln2_b': (0.0, 0.8),
     'L0_ffn_ln1_g': (1.0, 0.6),
     'L0_ffn_ln1_b': (0.0, 0.8),
     'L0_ffn_ln2_g': (1.0, 0.6),
     'L0_ffn_ln2_b': (0.0, 2.0),
     'L0_ffn_b1': (0.0, 2.0),
     'L0_ffn_b2': (0.0, 2.0)}
    factors = {'L0_attn_time_decay': 5.676,
     'L0_attn_time_first': 8.0,
     'L0_attn_time_mix_k': 8.0,
     'L0_attn_time_mix_v': 8.0,
     'L0_attn_time_mix_r': 8.0,
     'L0_attn_att_Wk': 8.0,
     'L0_attn_att_Wv': 4.036,
     'L0_attn_att_Wr': 8.0,
     'L0_attn_att_Wo': 4.038,
     'L0_attn_cm_k': 5.855,
     'L0_attn_cm_r': 8.0,
     'L0_attn_ffn_Wk': 3.991,
     'L0_attn_ffn_Wr': 8.0,
     'L0_attn_ffn_Wv': 3.574,
     'L0_ffn_Wq': 8.0,
     'L0_ffn_Wk': 8.0,
     'L0_ffn_Wv': 8.0,
     'L0_ffn_Wo': 8.0,
     'L0_ffn_Wg': 3.605,
     'L0_ffn_W1': 7.588,
     'L0_ffn_W2': 3.701}
    for name, (base, spread) in spreads.items():
        noise = np.random.default_rng([zlib.crc32(name.encode()), seed]).standard_normal(out[name].shape)
        drawn = base * np.exp(spread * noise) if base else spread * noise
        out[name] = jnp.asarray(drawn.astype(out[name].dtype))
    for name, factor in factors.items():
        out[name] = (out[name] * factor).astype(out[name].dtype)
    return out
```

```python
from contextlib import ExitStack

import concourse.bass as bass
from concourse import mybir

F32 = mybir.dt.float32
BF16 = mybir.dt.bfloat16
I32 = mybir.dt.int32
ACT = mybir.ActivationFunctionType
ALU = mybir.AluOpType
AX = mybir.AxisListType

P = 128
B, T, C = 2, 2048, 256
HID = 1024
CH = C // P
CT = 256
NCHUNK = T // CT
W = B * CT
NQ = W // P
EPS = 1e-5
HEADS, DH = 16, 16
NPART = 3

VEC = ["attn_ln1_g", "attn_ln1_b", "attn_ln2_g", "attn_ln2_b", "time_decay", "time_first",
       "time_mix_k", "time_mix_v", "time_mix_r", "cm_k", "cm_r", "ffn_ln1_g", "ffn_ln1_b",
       "ffn_ln2_g", "ffn_ln2_b"]


def wait(eng, sem, count):
    if not (isinstance(count, int) and count <= 0):
        eng.wait_ge(sem, count)


def rwkv_phase(nc, x, vecs, w, out_scr):
    with ExitStack() as ctx:
        def sb(name, shape, dt=F32):
            return ctx.enter_context(nc.sbuf_tensor(name, shape, dt))

        def sem(name):
            return nc.alloc_semaphore(name)

        wk, wv, wr, wo = (sb(f"att_w{n}", [P, CH, C]) for n in "kvro")
        fr, qw, kw, vw = (sb(n, [P, CH, C]) for n in ("ffn_wr", "q_w", "k_w", "v_w"))
        fk = sb("ffn_wk", [P, CH, HID])
        fv = sb("ffn_wv", [P, HID // P, C])
        vec = sb("vec", [P, len(VEC), CH])
        omt = sb("one_minus_mix", [P, 5, CH])
        dec = sb("decay", [P, CH])
        decb = sb("decay_rows", [P, CH, CT])
        ident = sb("ident", [P, P])
        mhalf = sb("minus_half", [P, NQ])

        def col(name, d):
            n = VEC.index(name)
            return vec[:, n, d:d + 1]

        xin = sb("x_in", [P, NQ, C])
        h0 = [sb(f"x_norm{p}", [P, NQ, C]) for p in range(2)]
        st = sb("stats", [P, NQ, 6])
        mv = {n: sb(f"mean_var_{n}", [P, NQ, 2]) for n in ("0", "1", "2", "3", "4", "5")}
        rs = {n: sb(f"rstd_{n}", [P, NQ]) for n in mv}
        n1 = sb("n1", [P, NQ, C])
        xa = sb("xa", [P, CH, B, CT + 1])
        exps = sb("exps", [P, 4, CH, B, CT])
        mt = exps[:, 0:3]
        mx = sb("mixed", [P, 3, CH, B, CT])
        kk_, vv_, gate = (sb(n, [P, CH, B, CT]) for n in ("k", "v", "gate"))
        scan = sb("scan", [P, 3, CH, B, CT + 1])
        pp, aa, bb = (scan[:, n] for n in range(3))
        dd, ff = exps[:, 0:2], exps[:, 2:4]
        pm = sb("out_max", [P, CH, B, CT])
        ev = pm
        num = sb("num", [P, CH, B, CT])
        den = sb("den", [P, CH, B, CT])
        rw = sb("rwkv", [P, CH, B, CT])
        xres = sb("x_res", [P, NQ, C])
        x1 = sb("x1", [P, NQ, C])
        n2 = sb("n2", [P, NQ, C])
        xc = sb("xc", [P, CH, B, CT + 1])
        mx2 = sb("mixed2", [P, 2, CH, B, CT])
        rel = [sb(f"relu{p}", [P, W]) for p in range(2)]
        hid = sb("hidden", [P, HID // P, W])
        mt2 = hid[:, 0:4, :].rearrange("p (m d) (b t) -> p m d b t", m=2, b=B)
        sg = sb("sig", [P, NQ, C])
        x2 = sg
        X1, h1 = (sb(n + "_tile", [P, NQ, C]) for n in ("X1", "h1"))
        n3 = n2
        hT = mx2[:, 0].rearrange("p d b t -> p d (b t)")
        parts = sb("qk_parts", [P, 2, CH, NPART, W], BF16)
        rest = [sb(f"rest{p}", [P, W]) for p in range(2)]
        va = sb("v_aug", [P, NQ, HEADS, 2 * DH])

        psA = ctx.enter_context(nc.psum_tensor("psA", [P, 3, 512], F32))
        psB = ctx.enter_context(nc.psum_tensor("psB", [P, 5, 512], F32))
        tokB = psB[:, 0:2, :].rearrange("p a (q c) -> p (a q) c", c=C)
        tokR = psB[:, 2:4, :].rearrange("p a (q c) -> p (a q) c", c=C)

        s = {}

        def S(name):
            if name not in s:
                s[name] = sem("p1_" + name)
            return s[name]

        xr = x.rearrange("b (c h p) d -> c b p h d", h=CT // P, p=P)
        rows = {n: out_scr[n].rearrange("b (c h p) d -> c b p h d", h=CT // P, p=P) for n in ("X1", "h1")}
        var = out_scr["v_aug"].rearrange("b (c h) p n -> c b p h n", h=CT // P)
        pr = out_scr["parts"].rearrange("n r (d p) b (c t) -> n r c p d b t", p=P, t=CT)

        def tiles(b):
            return slice(b * NQ // B, (b + 1) * NQ // B)

        with nc.Block() as block:
            @block.sync
            def _(sp):
                def load_x(dst, i, name):
                    for b in range(B):
                        sp.dma_start(dst[:, tiles(b), :], xr[i, b]).then_inc(S(name), 16)

                load_x(xin, 0, "x_loaded")
                sp.dma_start(vec[:], vecs).then_inc(S("vec_loaded"), 16)
                for t, d in ((wk, "att_Wk"), (wv, "att_Wv"), (wr, "att_Wr")):
                    sp.dma_start(t[:], w[d].rearrange("(k p) n -> p k n", p=P)).then_inc(S("kvr_loaded"), 16)
                for t, d in ((wo, "att_Wo"), (fk, "ffn_Wk"),
                             (fv, "ffn_Wv"), (fr, "ffn_Wr"), (qw, "Wq"), (kw, "Wk"), (vw, "Wv")):
                    sp.dma_start(t[:], w[d].rearrange("(k p) n -> p k n", p=P)).then_inc(S("weights"), 16)
                load_x(xres, 0, "x_res_loaded")
                for i in (1, 2):
                    sp.wait_ge(S("x_read"), i)
                    load_x(xin, i, "x_loaded")

                def chunk(i):
                    if not (isinstance(i, int) and i >= NCHUNK - 3):
                        sp.wait_ge(S("x_read"), i + 3)
                        load_x(xin, i + 3, "x_loaded")
                    sp.wait_ge(S("X1"), i + 1)
                    for b in range(B):
                        sp.dma_start(rows["X1"][i, b], X1[:, tiles(b), :]).then_inc(S("X1_stored"), 16)
                    if not (isinstance(i, int) and i >= NCHUNK - 1):
                        load_x(xres, i + 1, "x_res_loaded")
                    sp.wait_ge(S("h1"), i + 1)
                    for b in range(B):
                        sp.dma_start(rows["h1"][i, b], h1[:, tiles(b), :]).then_inc(S("h1_stored"), 16)
                    sp.wait_ge(S("parts"), i + 1)
                    for n in range(2):
                        for r in range(NPART):
                            for d in range(CH):
                                sp.dma_start(pr[n, r, i, :, d], parts[:, n, d, r, :].rearrange(
                                    "p (b t) -> p b t", b=B)).then_inc(S("parts_stored"), 16)
                    sp.wait_ge(S("v_aug"), i + 1)
                    for b in range(B):
                        sp.dma_start(var[i, b], va[:, tiles(b)].rearrange("p h n m -> p h (n m)")).then_inc(
                            S("v_stored"), 16)

                chunk(0)
                with sp.Fori(1, NCHUNK - 3) as i:
                    chunk(i)
                for i in range(NCHUNK - 3, NCHUNK):
                    chunk(i)
                for n in ("X1", "h1", "v"):
                    sp.wait_ge(S(n + "_stored"), 16 * B * NCHUNK)
                sp.wait_ge(S("parts_stored"), 16 * NCHUNK * 2 * NPART * CH)

            def chunks(eng, step):
                step(-2, 0)
                step(-1, 1)
                step(0, 0)
                with eng.Fori(0, (NCHUNK - 4) // 2) as t:
                    step(2 * t + 1, 1)
                    step(2 * t + 2, 0)
                for i in range(NCHUNK - 3, NCHUNK):
                    step(i, i % 2)

            def exists(i):
                return not isinstance(i, int) or 0 <= i < NCHUNK

            @block.gpsimd
            def _(pool):
                pool.memset(ident[:], 0.0)
                pool.memset(mhalf[:], -0.5)
                pool.memset(xa[:], 0.0)
                pool.drain()
                pool.affine_select(out=ident[:], in_=ident[:], compare_op=ALU.not_equal, fill=1.0, base=0,
                                   pattern=[[-1, P]], channel_multiplier=1)
                pool.drain()
                pool.nop().then_inc(S("consts"), 1)

                def rstd(n, i):
                    if exists(i):
                        pool.wait_ge(S("stats" + n), i + 1)
                        pool.tensor_tensor(rs[n][:], rs[n][:], mhalf[:], ALU.pow).then_inc(S("rstd" + n), 1)

                def step(i, par):
                    rstd("0", i + 2)
                    rstd("1", i + 2)
                    if isinstance(i, int) and i == -2:
                        pool.memset(scan[:], 0.0)
                        pool.drain()
                        pool.memset(pp[:, :, :, CT:CT + 1], -1e38)
                        pool.drain()
                        pool.memset(xc[:], 0.0)
                        pool.memset(va[:], 1.0)
                        pool.drain()
                        pool.nop().then_inc(S("consts"), 1)
                    rstd("3", i)
                    rstd("4", i)
                    rstd("5", i)
                    rstd("2", i + 1)

                chunks(pool, step)

            @block.vector
            def _(v):
                def stats(n, src):
                    for q in range(NQ):
                        v.bn_stats(st[:, q, :], src[:, q, :])
                    v.drain()
                    for q in range(NQ):
                        v.bn_aggr(mv[n][:, q, :], st[:, q, :])
                    v.drain()
                    v.tensor_scalar(rs[n][:], mv[n][:, :, 1], EPS, None, ALU.add).then_inc(S("stats" + n), 1)

                def normalise(n, dst, src, i):
                    v.wait_ge(S("rstd" + n), i + 1)
                    for q in range(NQ):
                        ins = v.tensor_scalar(dst[:, q, :], src[:, q, :], mv[n][:, q, 0:1], rs[n][:, q:q + 1],
                                              ALU.subtract, ALU.mult)
                    return ins

                def layernorms(i, par):
                    v.wait_ge(S("x_loaded"), 32 * i + 32)
                    stats("0", xin)
                    normalise("0", h0[par], xin, i).then_inc(S("x_read"), 1)
                    v.drain()
                    stats("1", h0[par])
                    normalise("1", n1, h0[par], i).then_inc(S("n1"), 1)

                def mix(i):
                    v.wait_ge(S("mix_tmp"), i + 1)
                    for m, name in enumerate(("time_mix_k", "time_mix_v", "time_mix_r")):
                        for d in range(CH):
                            ins = v.scalar_tensor_tensor(mx[:, m, d], xa[:, d, :, 1:CT + 1], col(name, d),
                                                         mt[:, m, d], ALU.mult, ALU.add)
                    ins.then_inc(S("mixed"), 1)

                def wkv_exponents(i):
                    v.drain()
                    v.wait_ge(S("k"), i + 1)
                    v.tensor_copy(scan[:, :, :, :, 0], scan[:, :, :, :, CT])
                    v.drain()
                    for d in range(CH):
                        for b in range(B):
                            v.tensor_tensor_scan(pp[:, d, b, 1:], decb[:, d, :], kk_[:, d, b, :],
                                                 pp[:, d, b, 0:1], ALU.add, ALU.max)
                    v.drain()
                    for d in range(CH):
                        v.scalar_tensor_tensor(dd[:, 0, d], pp[:, d, :, 0:CT], dec[:, d:d + 1],
                                               pp[:, d, :, 1:], ALU.subtract, ALU.subtract)
                    v.tensor_tensor(dd[:, 1], kk_[:], pp[:, :, :, 1:], ALU.subtract).then_inc(S("dd"), 1)
                    for d in range(CH):
                        v.scalar_tensor_tensor(pm[:, d], kk_[:, d], col("time_first", d), pp[:, d, :, 0:CT],
                                               ALU.add, ALU.max)
                    v.drain()
                    for d in range(CH):
                        v.scalar_tensor_tensor(ff[:, 1, d], kk_[:, d], col("time_first", d), pm[:, d],
                                               ALU.add, ALU.subtract)
                    v.tensor_tensor(ff[:, 0], pp[:, :, :, 0:CT], pm[:], ALU.subtract).then_inc(S("ff"), 1)

                def mix2(i):
                    v.wait_ge(S("mix2_tmp"), i + 1)
                    for m, name in enumerate(("cm_k", "cm_r")):
                        for d in range(CH):
                            ins = v.scalar_tensor_tensor(mx2[:, m, d], xc[:, d, :, 1:CT + 1], col(name, d),
                                                         mt2[:, m, d], ALU.mult, ALU.add)
                    ins.then_inc(S("mixed2"), 1)

                def wkv_output(i):
                    v.drain()
                    v.wait_ge(S("v"), i + 1)
                    v.wait_ge(S("dd_exp"), i + 1)
                    v.tensor_tensor(ev[:], dd[:, 1], vv_[:], ALU.mult)
                    for d in range(CH):
                        for b in range(B):
                            v.tensor_tensor_scan(bb[:, d, b, 1:], dd[:, 0, d, b], dd[:, 1, d, b],
                                                 bb[:, d, b, 0:1], ALU.mult, ALU.add)
                    v.drain()
                    for d in range(CH):
                        for b in range(B):
                            v.tensor_tensor_scan(aa[:, d, b, 1:], dd[:, 0, d, b], ev[:, d, b],
                                                 aa[:, d, b, 0:1], ALU.mult, ALU.add)
                    v.drain()
                    v.wait_ge(S("ff_exp"), i + 1)
                    v.tensor_tensor(den[:], ff[:, 0], bb[:, :, :, 0:CT], ALU.mult)
                    v.drain()
                    v.tensor_tensor(num[:], ff[:, 0], aa[:, :, :, 0:CT], ALU.mult)
                    v.tensor_tensor(den[:], den[:], ff[:, 1], ALU.add)
                    v.drain()
                    v.tensor_tensor(ev[:], ff[:, 1], vv_[:], ALU.mult)
                    v.reciprocal(den[:], den[:])
                    v.drain()
                    v.tensor_tensor(num[:], num[:], ev[:], ALU.add)
                    v.wait_ge(S("gate"), i + 1)
                    v.tensor_tensor(den[:], den[:], gate[:], ALU.mult)
                    v.drain()
                    v.tensor_tensor(rw[:], num[:], den[:], ALU.mult).then_inc(S("rw"), 1)

                def channel_mix_out(i):
                    v.wait_ge(S("sig"), i + 1)
                    v.wait_ge(S("kv"), i + 1)
                    v.tensor_tensor(x2[:], sg[:], tokB, ALU.mult).then_inc(S("kv_read"), 1)
                    v.drain()
                    v.tensor_tensor(x2[:], x2[:], x1[:], ALU.add)
                    v.drain()
                    stats("3", x2)
                    normalise("3", x2, x2, i)

                def outer_residual(i):
                    v.drain()
                    v.wait_ge(S("x_res_loaded"), 32 * i + 32)
                    wait(v, S("X1_stored"), 32 * i)
                    v.tensor_tensor(X1[:], x2[:], xres[:], ALU.add).then_inc(S("X1"), 1)
                    v.drain()
                    stats("4", X1)
                    wait(v, S("h1_stored"), 32 * i)
                    normalise("4", h1, X1, i).then_inc(S("h1"), 1)
                    v.drain()
                    stats("5", h1)
                    normalise("5", n3, h1, i).then_inc(S("n3"), 1)

                def time_mix_residual(i, par):
                    v.drain()
                    v.wait_ge(S("att_out"), i + 1)
                    v.tensor_tensor(x1[:], tokB, h0[par][:], ALU.add).then_inc(S("x1"), 1)
                    v.drain()
                    stats("2", x1)

                def split(i, m):
                    n, d = m // 2, m % 2
                    v.wait_ge(S("part0"), 4 * i + m + 1)
                    v.tensor_tensor(rest[m % 2][:], psB[:, 2 + m % 3, :], parts[:, n, d, 0, :],
                                    ALU.subtract).then_inc(S("rest"), 1)
                    v.wait_ge(S("part1"), 4 * i + m + 1)
                    return v.tensor_tensor(parts[:, n, d, 2, :], rest[m % 2][:], parts[:, n, d, 1, :],
                                           ALU.subtract)

                def step(i, par):
                    if exists(i + 1):
                        wkv_exponents(i + 1)
                    if exists(i):
                        mix2(i)
                    if exists(i + 1):
                        wkv_output(i + 1)
                    if exists(i + 2):
                        layernorms(i + 2, par)
                        if isinstance(i, int) and i == -2:
                            constants()
                    if exists(i):
                        channel_mix_out(i)
                    if exists(i + 2):
                        mix(i + 2)
                    if exists(i):
                        outer_residual(i)
                    if exists(i + 1):
                        time_mix_residual(i + 1, 1 - par)
                    if exists(i):
                        split(i, 0)
                        split(i, 1)
                    if exists(i + 1):
                        normalise("2", n2, x1, i + 1).then_inc(S("n2"), 1)
                    if exists(i):
                        split(i, 2)
                        split(i, 3).then_inc(S("parts"), 1)

                def constants():
                    v.wait_ge(S("vec_loaded"), 16)
                    for n, name in enumerate(("time_mix_k", "time_mix_v", "time_mix_r", "cm_k", "cm_r")):
                        ins = v.tensor_scalar(omt[:, n, :], vec[:, VEC.index(name), :], -1.0, 1.0, ALU.mult, ALU.add)
                    ins.then_inc(S("omt"), 1)
                    v.memset(decb[:], 0.0)
                    v.wait_ge(S("decay"), 1)
                    v.drain()
                    for d in range(CH):
                        v.tensor_scalar(decb[:, d, :], decb[:, d, :], dec[:, d:d + 1], None, ALU.subtract)
                    v.drain()
                    v.wait_ge(S("consts"), 2)

                chunks(v, step)

            @block.scalar
            def _(act):
                act.wait_ge(S("vec_loaded"), 16)
                act.activation(dec[:], vec[:, VEC.index("time_decay"), :], ACT.Exp).then_inc(S("decay"), 1)
                act.wait_ge(S("consts"), 2)

                def transposed(dst, g, b, src, i, name, bank):
                    act.wait_ge(S(name), i + 1)
                    act.copy(dst[:, :, :, 0], dst[:, :, :, CT])
                    act.drain()
                    for d in range(CH):
                        act.activation(dst[:, d, :, 1:], src[:, bank + d, :].rearrange("p (b t) -> p b t", b=B),
                                       ACT.Identity, scale=col(g, d), bias=col(b, d))
                    act.drain()

                def mix2_tmp(i):
                    transposed(xc, "attn_ln2_g", "attn_ln2_b", psB, i, "n2T", 2)
                    for m in range(2):
                        for d in range(CH):
                            ins = act.activation(mt2[:, m, d], xc[:, d, :, 0:CT], ACT.Copy,
                                                 scale=omt[:, 3 + m, d:d + 1])
                    ins.then_inc(S("mix2_tmp"), 1)

                def exponentials(i):
                    act.wait_ge(S("dd"), i + 1)
                    act.activation(dd[:], dd[:], ACT.Exp).then_inc(S("dd_exp"), 1)
                    act.wait_ge(S("ff"), i + 1)
                    act.activation(ff[:], ff[:], ACT.Exp).then_inc(S("ff_exp"), 1)

                def hidden(i):
                    for h in range(HID // P):
                        act.wait_ge(S("hid_psum"), 8 * i + h + 1)
                        act.activation(rel[h % 2][:], psB[:, 2 + h % 3, :], ACT.Relu).then_inc(S("relu"), 1)
                        act.drain()
                        act.activation(hid[:, h, :], rel[h % 2][:], ACT.Square).then_inc(S("hid"), 1)
                    act.wait_ge(S("r2"), i + 1)
                    act.activation(sg[:], tokR, ACT.Sigmoid).then_inc(S("sig"), 1)

                def mix_tmp(i):
                    transposed(xa, "attn_ln1_g", "attn_ln1_b", psA, i, "n1T", 0)
                    wait(act, S("rw"), i)
                    for m in range(3):
                        for d in range(CH):
                            ins = act.activation(mt[:, m, d], xa[:, d, :, 0:CT], ACT.Copy, scale=omt[:, m, d:d + 1])
                    ins.then_inc(S("mix_tmp"), 1)

                def projections(i):
                    for m, (dst, name) in enumerate(((kk_, "k"), (vv_, "v"), (gate, "gate"))):
                        for d in range(CH):
                            act.wait_ge(S("proj"), 6 * i + 2 * m + d + 1)
                            act.activation(dst[:, d].rearrange("p b t -> p (b t)"), psA[:, (2 * m + d) % 3, :],
                                           ACT.Sigmoid if m == 2 else ACT.Copy).then_inc(S("proj_read"), 1)
                        act.drain()
                        act.nop().then_inc(S(name), 1)

                def qkv(i):
                    act.wait_ge(S("n3T"), i + 1)
                    for d in range(CH):
                        ins = act.activation(hT[:, d, :], psB[:, 2 + d, :], ACT.Identity,
                                             scale=col("ffn_ln1_g", d), bias=col("ffn_ln1_b", d))
                    ins.then_inc(S("hT"), 1)
                    wait(act, S("parts_stored"), 16 * 12 * i)
                    for m in range(4):
                        n, d = m // 2, m % 2
                        act.wait_ge(S("qk"), 4 * i + m + 1)
                        act.activation(parts[:, n, d, 0, :], psB[:, 2 + m % 3, :], ACT.Copy).then_inc(
                            S("part0"), 1)
                        act.wait_ge(S("rest"), 4 * i + m + 1)
                        act.activation(parts[:, n, d, 1, :], rest[m % 2][:], ACT.Copy).then_inc(S("part1"), 1)
                    wait(act, S("v_stored"), 32 * i)
                    act.wait_ge(S("v_psum"), i + 1)
                    act.activation(va[:, :, :, 0:DH], tokB.rearrange("p q (n m) -> p q n m", m=DH),
                                   ACT.Copy).then_inc(S("v_aug"), 1)

                def step(i, par):
                    if exists(i):
                        mix2_tmp(i)
                    if exists(i + 1):
                        exponentials(i + 1)
                    if exists(i):
                        hidden(i)
                    if exists(i + 2):
                        mix_tmp(i + 2)
                        projections(i + 2)
                    if exists(i):
                        qkv(i)

                act.wait_ge(S("omt"), 1)
                chunks(act, step)

            @block.tensor
            def _(pe):
                pe.wait_ge(S("consts"), 1)

                def transposes(ps, bank, src):
                    for q in range(NQ):
                        for d in range(CH):
                            ins = pe.transpose(ps[:, bank + d, q * P:(q + 1) * P], src[:, q, d * P:(d + 1) * P],
                                               ident[:])
                    return ins

                def tokens(dst, lhs, rhs, n):
                    for q in range(NQ):
                        for k in range(n):
                            ins = pe.matmul(dst[:, q, :], lhs(k, q), rhs[:, k, :], start=(k == 0), stop=(k == n - 1))
                    return ins

                def channel_mix(i):
                    pe.wait_ge(S("n2"), i + 1)
                    wait(pe, S("rest"), 4 * i)
                    transposes(psB, 2, n2).then_inc(S("n2T"), 1)
                    pe.wait_ge(S("mixed2"), i + 1)
                    for h in range(HID // P):
                        if h >= 3:
                            pe.wait_ge(S("relu"), 8 * i + h - 2)
                        for d in range(CH):
                            ins = pe.matmul(psB[:, 2 + h % 3, :], fk[:, d, h * P:(h + 1) * P],
                                            mx2[:, 0, d].rearrange("p b t -> p (b t)"),
                                            start=(d == 0), stop=(d == CH - 1))
                        ins.then_inc(S("hid_psum"), 1)
                    pe.wait_ge(S("relu"), 8 * i + 8)
                    fl = mx2.rearrange("p m d b t -> p m d (b t)")
                    tokens(tokR, lambda k, q: fl[:, 1, k, q * P:(q + 1) * P], fr, CH).then_inc(S("r2"), 1)
                    pe.wait_ge(S("hid"), 8 * i + 8)
                    wait(pe, S("v_aug"), i)
                    tokens(tokB, lambda k, q: hid[:, k, q * P:(q + 1) * P], fv, HID // P).then_inc(S("kv"), 1)

                def projections(i):
                    pe.wait_ge(S("n1"), i + 1)
                    wait(pe, S("proj_read"), 6 * i)
                    transposes(psA, 0, n1).then_inc(S("n1T"), 1)
                    pe.wait_ge(S("mixed"), i + 1)
                    for m, wt in enumerate((wk, wv, wr)):
                        for o in range(CH):
                            j = 2 * m + o
                            if j >= 3:
                                pe.wait_ge(S("proj_read"), 6 * i + j - 2)
                            for d in range(CH):
                                ins = pe.matmul(psA[:, j % 3, :], wt[:, d, o * P:(o + 1) * P],
                                                mx[:, m, d].rearrange("p b t -> p (b t)"),
                                                start=(d == 0), stop=(d == CH - 1))
                            ins.then_inc(S("proj"), 1)

                def attention_out(i):
                    wait(pe, S("kv_read"), i)
                    pe.wait_ge(S("rw"), i + 1)
                    flat = rw.rearrange("p d b t -> p d (b t)")
                    tokens(tokB, lambda k, q: flat[:, k, q * P:(q + 1) * P], wo, CH).then_inc(S("att_out"), 1)

                def qkv(i, last):
                    pe.wait_ge(S("n3"), i + 1)
                    pe.wait_ge(S("sig"), i + 1)
                    transposes(psB, 2, n3).then_inc(S("n3T"), 1)
                    pe.wait_ge(S("hT"), i + 1)
                    for m in range(4):
                        wt, o = (qw, kw)[m // 2], m % 2
                        if m == 3:
                            pe.wait_ge(S("rest"), 4 * i + 1)
                        for d in range(CH):
                            ins = pe.matmul(psB[:, 2 + m % 3, :], wt[:, d, o * P:(o + 1) * P], hT[:, d, :],
                                            start=(d == 0), stop=(d == CH - 1))
                        ins.then_inc(S("qk"), 1)
                    if last:
                        pe.wait_ge(S("kv_read"), i + 1)
                    else:
                        pe.wait_ge(S("x1"), i + 2)
                    tokens(tokB, lambda k, q: hT[:, k, q * P:(q + 1) * P], vw, CH).then_inc(S("v_psum"), 1)

                def step(i, par):
                    if isinstance(i, int) and i == -2:
                        pe.wait_ge(S("kvr_loaded"), 16 * 3)
                    if exists(i):
                        channel_mix(i)
                    if exists(i + 2):
                        projections(i + 2)
                    if isinstance(i, int) and i == -1:
                        pe.wait_ge(S("weights"), 16 * 7)
                    if exists(i + 1):
                        attention_out(i + 1)
                    if exists(i):
                        qkv(i, not exists(i + 1))

                chunks(pe, step)

        nc.clear_and_free_semaphores(list(s.values()))
        nc.all_engine_barrier()


GROUPS = HEADS // 4
UNITS = B * GROUPS
QW = 512
NWIN = UNITS * (T // QW)
KT = T // P
KPARTS = (0, 1, 2, 0, 1, 0)
QPARTS = (0, 0, 0, 1, 1, 2)
ROWS = DH * len(KPARTS)
AHEAD = 4


def attention_phase(nc, scr):
    with ExitStack() as ctx:
        def sb(name, shape, dt=F32):
            return ctx.enter_context(nc.sbuf_tensor(name, shape, dt))

        kst = sb("k_stack", [P, 2, 4, T], BF16)
        qst = sb("q_stack", [P, 2, T // QW, 4, QW], BF16)
        vt = sb("v_tiles", [P, KT, P])
        pb = [sb(f"probs{p}", [P, 4, QW]) for p in range(2)]
        pmx = sb("part_max", [P, 16, 4])
        nmf = sb("neg_max", [P, 16])
        nmr = sb("neg_max_rest", [P, 16])
        nm3 = sb("neg_max_parts", [P, P // 16, 16], BF16)
        nmT = sb("neg_max_rows", [NPART * 16, P], BF16)
        csb = sb("ctx_sums", [P, QW])
        idb = sb("ident_bf", [P, P], BF16)

        psS = ctx.enter_context(nc.psum_tensor("ps_scores_t", [P, 4, QW], F32))
        psM = ctx.enter_context(nc.psum_tensor("ps_scores", [P, 2, QW], F32))
        psC = ctx.enter_context(nc.psum_tensor("ps_ctx", [P, QW], F32))
        psT = ctx.enter_context(nc.psum_tensor("ps_neg_max", [P, 1024], BF16))
        s = {}

        def S(name):
            if name not in s:
                s[name] = nc.alloc_semaphore("p2_" + name)
            return s[name]

        src = scr["parts"].rearrange("n r (g h d) b t -> n r b g d h t", g=GROUPS, h=4)
        vsrc = scr["v_aug"].rearrange("b (c k) p (g n) -> b g c p k n", c=4, g=GROUPS)
        cdst = scr["ctx"]
        NLOAD = 5 * len(KPARTS)

        with nc.Block() as block:
            @block.sync
            def _(sp):
                def load_qk(b, g, par):
                    for blk in range(len(KPARTS)):
                        r = slice(DH * blk, DH * blk + DH)
                        sp.dma_start(kst[r, par], src[1, KPARTS[blk], b, g]).then_inc(S("qk_loaded"), 16)
                        for h in range(4):
                            sp.dma_start(qst[r, par, :, h, :], src[0, QPARTS[blk], b, g, :, h].rearrange(
                                "d (c t) -> d c t", t=QW)).then_inc(S("qk_loaded"), 16)

                def load_v(b, g, c):
                    sp.dma_start(vt[:, 4 * c:4 * c + 4, :], vsrc[b, g, c]).then_inc(S(f"v_loaded{c}"), 16)

                def neg_max(w, qc, par):
                    sp.wait_ge(S("nmT"), w + 1)
                    for r in range(NPART):
                        sp.dma_start(qst[ROWS + r:ROWS + r + 1, par, qc].rearrange("a h t -> a (h t)").rearrange("a (n t) -> a n t", t=P),
                                     nmT[16 * r:16 * r + 16, :]).then_inc(S("neg_max"), 16)

                def unit(b, g, u, par, nxt):
                    if nxt:
                        if not isinstance(u, int) or u > 0:
                            sp.wait_ge(S("pv"), 2 + 64 * u)
                        load_qk(*nxt, 1 - par)
                    for qc in range(3):
                        neg_max(4 * u + qc + 1, qc + 1, par)
                    if nxt:
                        for c in range(4):
                            if c == 3:
                                neg_max(4 * u + 4, 0, 1 - par)
                            sp.wait_ge(S("pv"), 2 + 64 * u + 48 + 4 * c + 4)
                            load_v(*nxt, c)

                load_qk(0, 0, 0)
                for c in range(4):
                    load_v(0, 0, c)
                neg_max(0, 0, 0)
                unit(0, 0, 0, 0, (0, 1))
                unit(0, 1, 1, 1, (0, 2))
                unit(0, 2, 2, 0, (0, 3))
                unit(0, 3, 3, 1, (1, 0))
                unit(1, 0, 4, 0, (1, 1))
                unit(1, 1, 5, 1, (1, 2))
                unit(1, 2, 6, 0, (1, 3))
                unit(1, 3, 7, 1, None)

            def windows(eng, window):
                window(0, first=True)
                with eng.Fori(1, NWIN - 2) as w:
                    window(w)
                window(NWIN - 2, left=1)
                window(NWIN - 1, left=0)

            def job_of(w, kt, left):
                if kt < 16 - AHEAD:
                    return (w + 1, kt + AHEAD) if left > 0 else None
                return (w + 2, kt - 16 + AHEAD) if left > 1 else None

            @block.tensor
            def _(pe):
                pe.nop().then_inc(S("pv"), 2)
                pe.wait_ge(S("ones"), 1)
                pe.wait_ge(S("exp"), 2)
                pe.wait_ge(S("max_read"), 2)

                def job(mn, c):
                    if mn is None:
                        return
                    m, n = mn
                    h, q = n // 4, n % 4
                    par, qc = (m // 4) % 2, m % 4
                    if c == 0 and n == 0:
                        pe.wait_ge(S("qk_loaded"), 16 * NLOAD * (m // 4) + 16 * NLOAD)
                    pe.wait_ge(S("max_read"), 64 * m + 4 * n + c + 1)
                    pe.matmul(psM[:, c % 2, :], qst[0:ROWS, par, qc, h, q * P:(q + 1) * P],
                              kst[0:ROWS, par, h, c * QW:(c + 1) * QW], start=True, stop=True).then_inc(
                        S("max_scores"), 1)

                def scores(w, kt, p):
                    par, qc = (w // 4) % 2, w % 4
                    pe.wait_ge(S("exp"), 32 * w + 2 * kt + p + 1)
                    for h in range(2 * p, 2 * p + 2):
                        ins = pe.matmul(psS[:, h, :], kst[0:ROWS + NPART, par, h, kt * P:(kt + 1) * P],
                                        qst[0:ROWS + NPART, par, qc, h, :], start=True, stop=True)
                    ins.then_inc(S("scores"), 1)

                def values(w, kt):
                    if kt % 4 == 0:
                        pe.wait_ge(S(f"v_loaded{kt // 4}"), 16 * (w // 4) + 16)
                    if kt == 0:
                        wait(pe, S("ctx_read"), w)
                    pe.wait_ge(S("exp"), 32 * w + 2 * kt + 4)
                    for h in range(4):
                        ins = pe.matmul(psC[32 * h:32 * h + 32, :], vt[:, kt, 32 * h:32 * h + 32],
                                        pb[kt % 2][:, h, :], start=(kt == 0), stop=(kt == KT - 1))
                    ins.then_inc(S("pv"), 1)

                def turn_max(m):
                    pe.wait_ge(S("neg_max_parts"), m + 1)
                    pe.transpose(psT[:, 0:P], nm3.rearrange("p r n -> p (r n)"), idb[:]).then_inc(
                        S("neg_max_turned"), 1)

                for n in range(16 + AHEAD):
                    for c in range(4):
                        job((n // 16, n % 16), c)
                    if n == 15:
                        turn_max(0)

                def window(w, first=False, left=2):
                    pe.wait_ge(S("neg_max"), 48 * w + 48)
                    for kt in range(KT):
                        mn = job_of(w, kt, left)
                        job(mn, 0)
                        scores(w, kt, 0)
                        job(mn, 1)
                        scores(w, kt, 1)
                        job(mn, 2)
                        if kt == 16 - AHEAD and left:
                            turn_max(w + 1)
                        if kt > 0:
                            values(w, kt - 1)
                        elif not first:
                            values(w - 1, KT - 1)
                        job(mn, 3)

                windows(pe, window)
                values(NWIN - 1, KT - 1)

            @block.scalar
            def _(act):
                act.nop().then_inc(S("exp"), 2)

                def context(w):
                    act.wait_ge(S("sums_free"), w + 1)
                    act.wait_ge(S("pv"), 2 + 16 * w + 16)
                    act.copy(csb[:], psC[:]).then_inc(S("ctx_read"), 1)

                def window(w, first=False, left=2):
                    for kt in range(KT):
                        act.wait_ge(S("pv"), 16 * w + kt + 1)
                        for p in range(2):
                            act.wait_ge(S("scores"), 32 * w + 2 * kt + p + 1)
                            act.activation(pb[kt % 2][:, 2 * p:2 * p + 2, :], psS[:, 2 * p:2 * p + 2, :], ACT.Exp,
                                           scale=DH ** -0.5).then_inc(S("exp"), 1)
                        if kt == 0 and not first:
                            context(w - 1)

                windows(act, window)
                context(NWIN - 1)

            @block.vector
            def _(v):
                v.nop().then_inc(S("max_read"), 2)
                v.wait_ge(S("ones"), 1)

                def job(m, n):
                    for c in range(4):
                        v.wait_ge(S("max_scores"), 64 * m + 4 * n + c + 1)
                        v.tensor_reduce(pmx[:, n, c:c + 1], psM[:, c % 2, :], AX.X, ALU.max).then_inc(
                            S("max_read"), 1)

                def neg_max(m):
                    v.wait_ge(S("max_read"), 64 * m + 66)
                    v.tensor_reduce(nmf[:], pmx[:], AX.X, ALU.max, negate=True)
                    v.drain()
                    v.tensor_copy(nm3[:, 0, :], nmf[:])
                    v.drain()
                    v.tensor_tensor(nmr[:], nmf[:], nm3[:, 0, :], ALU.subtract)
                    v.drain()
                    v.tensor_copy(nm3[:, 1, :], nmr[:])
                    v.drain()
                    v.tensor_tensor(nm3[:, 2, :], nmr[:], nm3[:, 1, :], ALU.subtract).then_inc(
                        S("neg_max_parts"), 1)

                def neg_max_rows(m):
                    wait(v, S("neg_max"), 48 * m)
                    v.wait_ge(S("neg_max_turned"), m + 1)
                    v.tensor_copy(nmT[:], psT[0:NPART * 16, 0:P]).then_inc(S("nmT"), 1)

                for n in range(16 + AHEAD):
                    job(n // 16, n % 16)
                    if n == 15:
                        neg_max(0)
                neg_max_rows(0)

                def window(w, first=False, left=2):
                    for kt in range(KT):
                        mn = job_of(w, kt, left)
                        if mn:
                            job(*mn)
                        if kt == 15 - AHEAD and left:
                            neg_max(w + 1)
                        if kt == 16 - AHEAD and left:
                            neg_max_rows(w + 1)

                windows(v, window)

            @block.gpsimd
            def _(pool):
                pool.memset(kst[ROWS:ROWS + 32], 1.0)
                pool.drain()
                pool.memset(nm3[:], 0.0)
                pool.drain()
                pool.memset(idb[:], 0.0)
                pool.drain()
                pool.affine_select(out=idb[:], in_=idb[:], compare_op=ALU.not_equal, fill=1.0, base=0,
                                   pattern=[[-1, P]], channel_multiplier=1)
                pool.drain()
                pool.nop().then_inc(S("ones"), 1)
                pool.nop().then_inc(S("sums_free"), 1)
                with pool.Fori(0, NWIN) as w:
                    pool.wait_ge(S("ctx_read"), w + 1)
                    pool.dma_start(cdst[w], csb[:]).then_inc(S("ctx_stored"), 16)
                    pool.wait_ge(S("ctx_stored"), 16 * w + 16)
                    pool.nop().then_inc(S("sums_free"), 1)


E_ = 8
F = 1024
TB = T // P
NT = 2 * TB + E_ - 1
LN_EPS = EPS


def route_phase(nc, b, w, vec, scr, xn, slot, wts, eid):
    with ExitStack() as ctx:
        def sb(name, shape, dt=F32):
            return ctx.enter_context(nc.sbuf_tensor(f"r{b}_{name}", shape, dt))

        s = {}

        def S(name):
            if name not in s:
                s[name] = nc.alloc_semaphore(f"r{b}_{name}")
            return s[name]

        wo = sb("wo", [P, GROUPS, C])
        wg = sb("wg", [P, CH, E_])
        ident = sb("ident", [P, P])
        ones = sb("ones", [P, P])
        below = sb("below", [P, P])
        mhalf = sb("minus_half", [P, NQ])
        iota_i = sb("iota_i", [P, NT], I32)
        iota = sb("iota", [P, NT])
        rsum = sb("row_sums", [T // QW * HEADS, QW])
        rbc = sb("inv_sums", [P, GROUPS, QW])
        cx = sb("ctx", [P, GROUPS, QW])
        h1 = sb("h1", [P, NQ, C])
        xo = sb("x_mid", [P, NQ, C])
        st = sb("stats", [P, NQ, 6])
        mv = sb("mean_var", [P, NQ, 2])
        rs = sb("rstd", [P, NQ])
        n_tile = sb("n_tile", [P, NQ, C])
        mT = sb("mT", [P, CH, W])
        lg = sb("logits", [P, TB, E_])
        t8 = sb("top8", [P, TB, E_])
        i8 = sb("top8_idx", [P, TB, E_], mybir.dt.uint32)
        fi = sb("idx_f", [P, TB, E_])
        c1 = sb("choice", [P, TB])
        m12 = sb("one_hot", [P, 2, TB, E_])
        cnt = sb("count", [P, TB, E_])
        tot = sb("totals", [P, TB, E_])
        cum = sb("cum", [P, TB, E_])
        tl = sb("tile_tests", [P, E_, TB])
        te = sb("tiles_of_expert", [P, E_])
        tc = sb("tiles_cum", [P, E_])
        zero = sb("zero", [P, TB])
        off = sb("start", [P, E_])
        tmp = sb("tmp", [P, TB, E_])
        sf = sb("slot_f", [P, TB])
        ee = sb("expert_tests", [P, NT, E_ - 1])
        ef = sb("expert_f", [P, NT])
        ps = ctx.enter_context(nc.psum_tensor(f"r{b}_ps", [P, 6, 512], F32))
        tok = ps[:, 0:2, :].rearrange("p a (q c) -> p (a q) c", c=C)
        psl = ps[:, 4, 0:TB * E_].rearrange("p (n e) -> p n e", e=E_)
        psc = ps[:, 5, 0:2 * TB * E_].rearrange("p (k n e) -> p k n e", k=2, e=E_)

        sums = scr["ctx"].rearrange("(b g c) (h r) t -> b (g c) h r t", b=B, g=GROUPS, h=4)[b, :, :, DH, :]
        inv = scr["inv"][b]
        inv_v = inv.rearrange("(g c) h t -> c h g t", g=GROUPS)
        cin = scr["ctx"].rearrange("(b g c) p t -> b c p g t", b=B, g=GROUPS)[b]
        hin = scr["h1"].rearrange("b (c q p) d -> b c p q d", q=NQ, p=P)[b]
        xout = scr["x_mid"].rearrange("b (c q p) d -> b c p q d", q=NQ, p=P)[b]

        with nc.Block() as block:
            @block.sync
            def _(sp):
                for k in range(GROUPS * 4):
                    sp.dma_start(rsum[4 * k:4 * k + 4, :], sums[k]).then_inc(S("sums"), 16)
                sp.wait_ge(S("zeroed"), 1)
                for j in range(4):
                    sp.dma_start(wo[32 * j:32 * j + DH], w["Wo"].rearrange("(g j d) n -> j d g n", j=4, d=DH)[j]
                                 ).then_inc(S("weights"), 16)
                sp.dma_start(wg[:], w["Wg"].rearrange("(k p) n -> p k n", p=P)).then_inc(S("weights"), 16)
                sp.wait_ge(S("inv"), 1)
                sp.dma_start(inv.rearrange("k h t -> (k h) t"), rsum[:]).then_inc(S("inv_stored"), 16)
                sp.wait_ge(S("inv_stored"), 16)

                def load(c):
                    sp.dma_start(cx[:], cin[c]).then_inc(S("ctx"), 16)
                    for j in range(4):
                        sp.dma_start(rbc[32 * j:32 * j + 32], inv_v[c, j].partition_broadcast(32)).then_inc(
                            S("ctx"), 16)
                    sp.dma_start(h1[:], hin[c]).then_inc(S("ctx"), 16)

                load(0)
                for c in range(T // W):
                    sp.wait_ge(S("x_mid"), c + 1)
                    if c < T // W - 1:
                        load(c + 1)
                    sp.dma_start(xout[c], xo[:]).then_inc(S("x_stored"), 16)
                sp.wait_ge(S("x_stored"), 16 * T // W)

            @block.gpsimd
            def _(pool):
                pool.memset(wo[:], 0.0)
                pool.drain()
                pool.nop().then_inc(S("zeroed"), 1)
                pool.memset(ident[:], 0.0)
                pool.memset(ones[:], 1.0)
                pool.memset(mhalf[:], -0.5)
                pool.iota(iota_i[:], [[1, NT]], base=0, channel_multiplier=0)
                pool.drain()
                pool.affine_select(out=ident[:], in_=ident[:], compare_op=ALU.not_equal, fill=1.0, base=0,
                                   pattern=[[-1, P]], channel_multiplier=1)
                pool.affine_select(out=below[:], in_=ones[:], compare_op=ALU.is_gt, fill=0.0, base=0,
                                   pattern=[[1, P]], channel_multiplier=-1)
                pool.drain()
                pool.nop().then_inc(S("consts"), 1)
                with pool.Fori(0, T // W) as c:
                    pool.wait_ge(S("stats"), c + 1)
                    pool.tensor_tensor(rs[:], rs[:], mhalf[:], ALU.pow).then_inc(S("rstd"), 1)

            @block.tensor
            def _(pe):
                pe.wait_ge(S("weights"), 16 * 5)
                pe.wait_ge(S("consts"), 1)
                with pe.Fori(0, T // W) as c:
                    pe.wait_ge(S("scaled"), c + 1)
                    for q in range(NQ):
                        for g in range(GROUPS):
                            ins = pe.matmul(tok[:, q, :], cx[:, g, q * P:(q + 1) * P], wo[:, g, :],
                                            start=(g == 0), stop=(g == GROUPS - 1))
                    ins.then_inc(S("proj"), 1)
                    pe.wait_ge(S("norm"), c + 1)
                    for q in range(NQ):
                        for d in range(CH):
                            ins = pe.transpose(ps[:, 2 + d, q * P:(q + 1) * P], n_tile[:, q, d * P:(d + 1) * P],
                                               ident[:])
                    ins.then_inc(S("turned"), 1)
                    pe.wait_ge(S("mT"), c + 1)
                    for q in range(NQ):
                        for d in range(CH):
                            ins = pe.matmul(psl[:, q, :], mT[:, d, q * P:(q + 1) * P], wg[:, d, :],
                                            start=(d == 0), stop=(d == CH - 1))
                    ins.then_inc(S("logits"), 1)
                pe.wait_ge(S("count"), 1)
                flat = cnt.rearrange("p n e -> p (n e)")
                for k, m in enumerate((below, ones)):
                    ins = pe.matmul(ps[:, 5, k * TB * E_:(k + 1) * TB * E_], m[:], flat, start=True, stop=True)
                ins.then_inc(S("prefix"), 1)

            @block.scalar
            def _(act):
                with act.Fori(0, T // W) as c:
                    act.wait_ge(S("turned"), c + 1)
                    for d in range(CH):
                        ins = act.activation(mT[:, d, :], ps[:, 2 + d, :], ACT.Identity,
                                             scale=vec[:, VEC.index("ffn_ln2_g"), d:d + 1],
                                             bias=vec[:, VEC.index("ffn_ln2_b"), d:d + 1])
                    ins.then_inc(S("mT"), 1)
                act.wait_ge(S("shifted"), 1)
                act.activation(lg[:], lg[:], ACT.Exp).then_inc(S("exp"), 1)

            @block.vector
            def _(v):
                v.wait_ge(S("sums"), 16 * GROUPS * 4)
                v.reciprocal(rsum[:], rsum[:]).then_inc(S("inv"), 1)
                v.memset(zero[:], 0.0)
                v.wait_ge(S("consts"), 1)
                v.tensor_copy(iota[:], iota_i[:])
                def chunk(c):
                    v.wait_ge(S("ctx"), 96 * c + 96)
                    v.tensor_tensor(cx[:], cx[:], rbc[:], ALU.mult).then_inc(S("scaled"), 1)
                    wait(v, S("x_stored"), 16 * c)
                    v.wait_ge(S("proj"), c + 1)
                    v.tensor_tensor(xo[:], tok, h1[:], ALU.add).then_inc(S("x_mid"), 1)
                    v.drain()
                    for q in range(NQ):
                        v.bn_stats(st[:, q, :], xo[:, q, :])
                    v.drain()
                    for q in range(NQ):
                        v.bn_aggr(mv[:, q, :], st[:, q, :])
                    v.drain()
                    v.tensor_scalar(rs[:], mv[:, :, 1], LN_EPS, None, ALU.add).then_inc(S("stats"), 1)
                    v.wait_ge(S("rstd"), c + 1)
                    for q in range(NQ):
                        ins = v.tensor_scalar(n_tile[:, q, :], xo[:, q, :], mv[:, q, 0:1], rs[:, q:q + 1],
                                              ALU.subtract, ALU.mult)
                    ins.then_inc(S("norm"), 1)
                    v.drain()
                    v.tensor_copy(xn[:, bass.ds(NQ * c, NQ), :], n_tile[:])
                    v.wait_ge(S("logits"), c + 1)
                    v.tensor_copy(lg[:, bass.ds(NQ * c, NQ), :], psl[:, 0:NQ, :])

                chunk(0)
                with v.Fori(1, T // W) as c:
                    chunk(c)

                def wide(t):
                    return t.unsqueeze(2).to_broadcast([P, TB, E_])

                def rows(t):
                    return t.unsqueeze(1).to_broadcast([P, TB, E_])

                v.drain()
                v.tensor_reduce(c1[:], lg[:], AX.X, ALU.max)
                v.drain()
                v.tensor_tensor(lg[:], lg[:], wide(c1[:]), ALU.subtract).then_inc(S("shifted"), 1)
                v.wait_ge(S("exp"), 1)
                v.tensor_reduce(c1[:], lg[:], AX.X, ALU.add)
                v.drain()
                v.reciprocal(c1[:], c1[:])
                v.drain()
                v.tensor_tensor(lg[:], lg[:], wide(c1[:]), ALU.mult)
                v.drain()
                for n in range(TB):
                    v.max(t8[:, n, :], lg[:, n, :])
                v.drain()
                for n in range(TB):
                    v.max_index(i8[:, n, :], t8[:, n, :], lg[:, n, :])
                v.tensor_tensor(c1[:], t8[:, :, 0], t8[:, :, 1], ALU.add)
                v.drain()
                v.reciprocal(c1[:], c1[:])
                v.tensor_copy(fi[:], i8[:])
                v.drain()
                for k in range(2):
                    v.tensor_tensor(wts[:, :, k], t8[:, :, k], c1[:], ALU.mult)
                    v.tensor_tensor(m12[:, k], rows(iota[:, 0:E_]), wide(fi[:, :, k]), ALU.is_equal)
                v.drain()
                v.tensor_tensor(cnt[:], m12[:, 0], m12[:, 1], ALU.add).then_inc(S("count"), 1)
                v.wait_ge(S("prefix"), 1)
                v.tensor_copy(tot[:], psc[:, 1])
                v.drain()
                for e in range(E_):
                    v.tensor_tensor_scan(cum[:, :, e], tot[:, :, e], zero[:], 0.0, ALU.add, ALU.add)
                v.drain()
                v.tensor_scalar(tl[:, 0, :], iota[:, 0:TB], float(P), None, ALU.mult)
                v.drain()
                v.tensor_copy(c1[:], tl[:, 0, :])
                v.drain()
                v.tensor_tensor(tl[:], cum[:, TB - 1, :].unsqueeze(2).to_broadcast([P, E_, TB]),
                                c1[:].unsqueeze(1).to_broadcast([P, E_, TB]), ALU.is_gt)
                v.drain()
                v.tensor_reduce(te[:], tl[:], AX.X, ALU.add)
                v.drain()
                v.tensor_tensor_scan(tc[:], te[:], zero[:, 0:E_], 0.0, ALU.add, ALU.add)
                v.drain()
                v.tensor_tensor(off[:], tc[:], te[:], ALU.subtract)
                v.tensor_tensor(cum[:], cum[:], tot[:], ALU.subtract)
                v.drain()
                v.tensor_scalar(off[:], off[:], float(P), None, ALU.mult)
                v.tensor_tensor(cum[:], cum[:], psc[:, 0], ALU.add)
                v.drain()
                v.tensor_tensor(cum[:], cum[:], rows(off[:]), ALU.add)
                for k in range(2):
                    v.drain()
                    v.tensor_tensor(tmp[:], cum[:], m12[:, k], ALU.mult)
                    v.drain()
                    v.tensor_reduce(sf[:], tmp[:], AX.X, ALU.add)
                    v.drain()
                    v.tensor_copy(slot[:, :, k], sf[:])
                v.tensor_tensor(ee[:], iota[:].unsqueeze(2).to_broadcast([P, NT, E_ - 1]),
                                tc[:, 0:E_ - 1].unsqueeze(1).to_broadcast([P, NT, E_ - 1]), ALU.is_ge)
                v.drain()
                v.tensor_reduce(ef[:], ee[:], AX.X, ALU.add)
                v.drain()
                v.tensor_copy(eid[:], ef[:])


def expert_phase(nc, b, vec, ew, scr, eid, pool_work):
    w1, w2, b1, b2 = ew
    with ExitStack() as ctx:
        def sb(name, shape, dt=F32):
            return ctx.enter_context(nc.sbuf_tensor(f"e{b}_{name}", shape, dt))

        s = {}

        def S(name):
            if name not in s:
                s[name] = nc.alloc_semaphore(f"e{b}_{name}")
            return s[name]

        FT = F // P
        ident = sb("ident", [P, P])
        xs = sb("x_slots", [P, C])
        xT = sb("xT", [P, CH, P])
        pre = sb("pre", [P, F])
        g = sb("gelu", [P, F])
        hT = sb("hT", [P, FT, P])
        y = sb("y", [P, C])
        psU = ctx.enter_context(nc.psum_tensor(f"e{b}_up", [P, F], F32))
        psH = ctx.enter_context(nc.psum_tensor(f"e{b}_ht", [P, FT, P], F32))
        psX = ctx.enter_context(nc.psum_tensor(f"e{b}_xt", [P, CH, P], F32))
        psD = ctx.enter_context(nc.psum_tensor(f"e{b}_down", [P, C], F32))
        xin = scr["x_slots"][b].rearrange("(j p) d -> j p d", p=P)
        yout = scr["y_slots"][b].rearrange("(j p) d -> j p d", p=P)
        L = NT - 1

        def expert(eng, j):
            return eng.value_load(eid[0:1, j:j + 1] if isinstance(j, int) else eid[0:1, bass.ds(j, 1)],
                                  min_val=0, max_val=E_ - 1)

        with nc.Block() as block:
            @block.sync
            def _(sp):
                def load(j):
                    if not isinstance(j, int) or j > 0:
                        sp.wait_ge(S("x_turned"), j)
                    sp.dma_start(xs[:], xin[j]).then_inc(S("x_slots"), 16)

                def store(j):
                    sp.wait_ge(S("y"), j + 1)
                    sp.dma_start(yout[j], y[:]).then_inc(S("y_stored"), 16)

                load(0)
                load(1)
                with sp.Fori(1, L) as j:
                    load(j + 1)
                    store(j - 1)
                store(L - 1)
                store(L)
                sp.wait_ge(S("y_stored"), 16 * NT)

            @block.gpsimd
            def _(pool):
                pool.memset(ident[:], 0.0)
                pool.drain()
                pool.affine_select(out=ident[:], in_=ident[:], compare_op=ALU.not_equal, fill=1.0, base=0,
                                   pattern=[[-1, P]], channel_multiplier=1)
                pool.drain()
                pool.nop().then_inc(S("consts"), 1)
                pool_work(pool)

            @block.tensor
            def _(pe):
                def turn_x(j):
                    pe.wait_ge(S("x_slots"), 16 * j + 16)
                    wait(pe, S("xT"), j)
                    for d in range(CH):
                        ins = pe.transpose(psX[:, d, :], xs[:, d * P:(d + 1) * P], ident[:])
                    ins.then_inc(S("x_turned"), 1)

                def up(j):
                    e = expert(pe, j)
                    pe.wait_ge(S("xT"), j + 1)
                    wait(pe, S("biased"), j)
                    for h in range(F // 512):
                        for d in range(CH):
                            ins = pe.matmul(psU[:, h * 512:(h + 1) * 512], xT[:, d, :],
                                            w1[:, d, e, h * 512:(h + 1) * 512], start=(d == 0), stop=(d == CH - 1))
                    ins.then_inc(S("up"), 1)

                def turn_h(j):
                    pe.wait_ge(S("gelu"), j + 1)
                    for f in range(FT):
                        if f % 4 == 0:
                            wait(pe, S(f"hT{f // 4}"), j)
                        ins = pe.transpose(psH[:, f, :], g[:, f * P:(f + 1) * P], ident[:])
                        if f % 4 == 3:
                            ins.then_inc(S("h_turned"), 1)

                def down(j):
                    e = expert(pe, j)
                    wait(pe, S("y"), j)
                    for f in range(FT):
                        if f % 4 == 0:
                            pe.wait_ge(S(f"hT{f // 4}"), j + 1)
                        ins = pe.matmul(psD[:], hT[:, f, :], w2[:, f, e, :], start=(f == 0), stop=(f == FT - 1))
                    ins.then_inc(S("down"), 1)

                pe.wait_ge(S("consts"), 1)
                turn_x(0)
                up(0)
                turn_x(1)
                turn_h(0)

                def step(j):
                    up(j)
                    turn_x(j + 1)
                    down(j - 1)
                    turn_h(j)

                step(1)
                with pe.Fori(2, NT - 1) as j:
                    step(j)
                up(L)
                down(L - 1)
                turn_h(L)
                down(L)

            @block.scalar
            def _(act):
                def x_t(j):
                    act.wait_ge(S("x_turned"), j + 1)
                    wait(act, S("up"), j)
                    for d in range(CH):
                        ins = act.activation(xT[:, d, :], psX[:, d, :], ACT.Identity,
                                             scale=vec[:, VEC.index("ffn_ln2_g"), d:d + 1],
                                             bias=vec[:, VEC.index("ffn_ln2_b"), d:d + 1])
                    ins.then_inc(S("xT"), 1)

                def gelu(j):
                    act.wait_ge(S("biased"), j + 1)
                    act.activation(g[:], pre[:], ACT.Gelu_apprx_tanh).then_inc(S("gelu"), 1)

                def h_t(j):
                    act.wait_ge(S("h_turned"), 2 * j + 2)
                    act.copy(hT[:, FT // 2:, :], psH[:, FT // 2:, :]).then_inc(S("hT1"), 1)

                x_t(0)
                x_t(1)
                gelu(0)
                h_t(0)
                with act.Fori(1, NT - 1) as j:
                    x_t(j + 1)
                    gelu(j)
                    h_t(j)
                gelu(L)
                h_t(L)

            @block.vector
            def _(v):
                def bias(j):
                    e = expert(v, j)
                    wait(v, S("gelu"), j)
                    v.wait_ge(S("up"), j + 1)
                    v.tensor_tensor(pre[:], psU[:], b1[:, e, :], ALU.add).then_inc(S("biased"), 1)

                def h_t(j):
                    v.wait_ge(S("h_turned"), 2 * j + 1)
                    v.tensor_copy(hT[:, 0:FT // 2, :], psH[:, 0:FT // 2, :]).then_inc(S("hT0"), 1)

                def out(j):
                    e = expert(v, j)
                    wait(v, S("y_stored"), 16 * j)
                    v.wait_ge(S("down"), j + 1)
                    v.tensor_tensor(y[:], psD[:], b2[:, e, :], ALU.add).then_inc(S("y"), 1)

                bias(0)
                h_t(0)

                def step(j):
                    bias(j)
                    out(j - 1)
                    h_t(j)

                step(1)
                with v.Fori(2, NT) as j:
                    step(j)
                out(L)


def combine_phase(nc, scr, slot, wts, out):
    with ExitStack() as ctx:
        def sb(name, shape, dt=F32):
            return ctx.enter_context(nc.sbuf_tensor("c_" + name, shape, dt))

        s = {}

        def S(name):
            if name not in s:
                s[name] = nc.alloc_semaphore("c_" + name)
            return s[name]

        NB = 4
        ya, yb, xm, xo = ([sb(f"{n}{k}", [P, C]) for k in range(NB)] for n in ("ya", "yb", "x_mid", "x_outer"))
        st = [sb(f"stats{k}", [P, 6]) for k in range(NB)]
        mv = [sb(f"mean_var{k}", [P, 2]) for k in range(NB)]
        rs = [sb(f"rstd{k}", [P, 1]) for k in range(NB)]
        mhalf = sb("minus_half", [P, 1])
        xin = scr["x_mid"].rearrange("b (n p) d -> (b n) p d", p=P)
        oin = scr["X1"].rearrange("b (n p) d -> (b n) p d", p=P)
        dst = out.rearrange("b (n p) d -> (b n) p d", p=P)
        N = B * TB

        with nc.Block() as block:
            @block.sync
            def _(sp):
                for n in range(N + 2):
                    if n < N:
                        k = n % NB
                        if n >= NB:
                            sp.wait_ge(S(f"stored{k}"), 16 * (n // NB))
                        sp.dma_start(xm[k][:], xin[n]).then_inc(S(f"loaded{k}"), 16)
                        sp.dma_start(xo[k][:], oin[n]).then_inc(S(f"loaded{k}"), 16)
                    if n >= 2:
                        sp.wait_ge(S("done"), n - 1)
                        sp.dma_start(dst[n - 2], xo[(n - 2) % NB][:]).then_inc(S(f"stored{(n - 2) % NB}"), 16)
                for k in range(NB):
                    sp.wait_ge(S(f"stored{k}"), 16 * N // NB)

            @block.gpsimd
            def _(pool):
                pool.memset(mhalf[:], -0.5)
                pool.drain()

                def gather(n):
                    k = n % NB
                    if n >= NB:
                        pool.wait_ge(S("summed"), n - NB + 1)
                    for c, dst_ in enumerate((ya, yb)):
                        pool.indirect_dma_start(dst_[k][:], None, scr["y_slots"][n // TB], bass.IndirectOffsetOnAxis(
                            ap=slot[n // TB][:, n % TB, c:c + 1], axis=0)).then_inc(S(f"gathered{k}"), 16)

                gather(0)
                gather(1)
                for n in range(N):
                    if n + 2 < N:
                        gather(n + 2)
                    k = n % NB
                    pool.wait_ge(S("stats"), n + 1)
                    pool.tensor_tensor(rs[k][:], rs[k][:], mhalf[:], ALU.pow).then_inc(S("rstd"), 1)

            @block.vector
            def _(v):
                for n in range(N):
                    k, b = n % NB, n // TB
                    v.wait_ge(S(f"loaded{k}"), 32 * (n // NB) + 32)
                    v.wait_ge(S(f"gathered{k}"), 32 * (n // NB) + 32)
                    v.scalar_tensor_tensor(xm[k][:], ya[k][:], wts[b][:, n % TB, 0:1], xm[k][:], ALU.mult, ALU.add)
                    v.drain()
                    v.scalar_tensor_tensor(xm[k][:], yb[k][:], wts[b][:, n % TB, 1:2], xm[k][:], ALU.mult,
                                           ALU.add).then_inc(S("summed"), 1)
                    v.drain()
                    v.bn_stats(st[k][:], xm[k][:])
                    v.drain()
                    v.bn_aggr(mv[k][:], st[k][:])
                    v.drain()
                    v.tensor_scalar(rs[k][:], mv[k][:, 1:2], LN_EPS, None, ALU.add).then_inc(S("stats"), 1)
                    v.wait_ge(S("rstd"), n + 1)
                    v.tensor_scalar(xm[k][:], xm[k][:], mv[k][:, 0:1], rs[k][:], ALU.subtract, ALU.mult)
                    v.drain()
                    v.tensor_tensor(xo[k][:], xo[k][:], xm[k][:], ALU.add).then_inc(S("done"), 1)


def scatter_rows(pool, nc, b, xn, slot, scr, sem):
    for n in range(TB):
        for c in range(2):
            pool.indirect_dma_start(scr["x_slots"][b], bass.IndirectOffsetOnAxis(ap=slot[:, n, c:c + 1], axis=0),
                                    xn[:, n, :], None).then_inc(sem, 16)


def moe_layer(nc, w, vecs, scr, out):
    with ExitStack() as ctx:
        def sb(name, shape, dt=F32):
            return ctx.enter_context(nc.sbuf_tensor(name, shape, dt))

        vec = sb("moe_vec", [P, len(VEC), CH])
        slot = [sb(f"slot{b}", [P, TB, 2], I32) for b in range(B)]
        wts = [sb(f"weights{b}", [P, TB, 2]) for b in range(B)]
        eid = [sb(f"eid{b}", [P, NT], I32) for b in range(B)]
        with ExitStack() as inner:
            xn = [inner.enter_context(nc.sbuf_tensor(f"xn{b}", [P, TB, C], F32)) for b in range(B)]
            zero = inner.enter_context(nc.sbuf_tensor("zero_rows", [P, 13 * C], F32))
            done = nc.alloc_semaphore("zero_stored")
            zs = nc.alloc_semaphore("zero_ready")
            with nc.Block() as block:
                @block.gpsimd
                def _(pool):
                    pool.memset(zero[:], 0.0).then_inc(zs, 1)

                @block.sync
                def _(sp):
                    sp.dma_start(vec[:], vecs).then_inc(done, 16)
                    sp.wait_ge(zs, 1)
                    for b in range(B):
                        dst = scr["x_slots"][b].rearrange("(p t) d -> p (t d)", p=P)
                        for k in range(NT // 13):
                            sp.dma_start(dst[:, 13 * C * k:13 * C * (k + 1)], zero[:]).then_inc(done, 16)
                    sp.wait_ge(done, 16 * (B * NT // 13 + 1))
            for b in range(B):
                route_phase(nc, b, w, vec, scr, xn[b], slot[b], wts[b], eid[b])
            sc = nc.alloc_semaphore("scattered")
            with nc.Block() as block:
                @block.gpsimd
                def _(pool):
                    for b in range(B):
                        scatter_rows(pool, nc, b, xn[b], slot[b], scr, sc)
                    pool.wait_ge(sc, 16 * 2 * TB * B)
        with ExitStack() as inner:
            def isb(name, shape):
                return inner.enter_context(nc.sbuf_tensor("expert_" + name, shape, F32))

            w1 = isb("w1", [P, CH, E_, F])
            w2 = isb("w2", [P, F // P, E_, C])
            b1 = isb("b1", [P, E_, F])
            b2 = isb("b2", [P, E_, C])
            ld = nc.alloc_semaphore("experts_loaded")
            with nc.Block() as block:
                @block.sync
                def _(sp):
                    for e in range(E_):
                        sp.dma_start(w1[:, :, e, :], w["W1"][e].rearrange("(k p) n -> p k n", p=P)).then_inc(ld, 16)
                        sp.dma_start(w2[:, :, e, :], w["W2"][e].rearrange("(k p) n -> p k n", p=P)).then_inc(ld, 16)
                    sp.dma_start(b1[:], w["b1"].partition_broadcast(P)).then_inc(ld, 16)
                    sp.dma_start(b2[:], w["b2"].partition_broadcast(P)).then_inc(ld, 16)
                    sp.wait_ge(ld, 16 * (2 * E_ + 2))
            for b in range(B):
                expert_phase(nc, b, vec, (w1, w2, b1, b2), scr, eid[b], lambda pool: None)
        combine_phase(nc, scr, slot, wts, out)


INPUTS = {
    "x": "L0_attn_x",
    **{n: "L0_attn_" + n for n in ("att_Wk", "att_Wv", "att_Wr", "att_Wo", "ffn_Wk", "ffn_Wr", "ffn_Wv")},
    **{n: "L0_ffn_" + n for n in ("Wq", "Wk", "Wv", "Wo", "Wg", "W1", "b1", "W2", "b2")},
}
ATTN_VEC = {n: "L0_attn_" + n for n in ("time_decay", "time_first", "time_mix_k", "time_mix_v", "time_mix_r", "cm_k",
                                        "cm_r")}
ATTN_VEC.update({f"attn_ln{k}_{c}": f"L0_attn_ln{k}_{c}" for k in (1, 2) for c in "gb"})
ATTN_VEC.update({f"ffn_ln{k}_{c}": f"L0_ffn_ln{k}_{c}" for k in (1, 2) for c in "gb"})


def sandwich(nc, w, out):
    def scratch(name, shape, dt=F32):
        return nc.dram_tensor("scr_" + name, shape, dt, kind="Internal").ap()

    scr = {
        "X1": scratch("X1", (B, T, C)),
        "h1": scratch("h1", (B, T, C)),
        "v_aug": scratch("v_aug", (B, T // P, P, HEADS * 2 * DH)),
        "parts": scratch("parts", (2, NPART, C, B, T), BF16),
        "ctx": scratch("ctx", (NWIN, P, QW)),
        "inv": scratch("inv", (B, T // QW * GROUPS, 4, QW)),
        "x_mid": scratch("x_mid", (B, T, C)),
        "x_slots": [scratch(f"x_slots{b}", (NT * P, C)) for b in range(B)],
        "y_slots": [scratch(f"y_slots{b}", (NT * P, C)) for b in range(B)],
    }
    rwkv_phase(nc, w["x"], w["vecs"], w, scr)
    attention_phase(nc, scr)
    moe_layer(nc, w, w["vecs"], scr, out)


def kernel(**inputs):
    import numpy as np
    import concourse.bacc as bacc
    from concourse.bass_utils import run_bass_kernel_spmd

    arrays = {n: np.ascontiguousarray(inputs[k]) for n, k in INPUTS.items()}
    for n in ("att_Wk", "att_Wv", "att_Wr", "att_Wo", "ffn_Wk", "ffn_Wr", "ffn_Wv"):
        arrays[n] = np.ascontiguousarray(np.asarray(inputs[INPUTS[n]]).T)
    vecs = np.stack([np.asarray(inputs[ATTN_VEC[n]]) for n in VEC])
    arrays["vecs"] = np.ascontiguousarray(vecs.reshape(len(VEC), CH, P).transpose(2, 0, 1))
    nc = bacc.Bacc("TRN2", target_bir_lowering=False, num_devices=1)
    w = {n: nc.dram_tensor(f"in_{n}", a.shape, mybir.dt.from_np(a.dtype), kind="ExternalInput").ap()
         for n, a in arrays.items()}
    out = nc.dram_tensor("out_x", (B, T, C), F32, kind="ExternalOutput").ap()
    sandwich(nc, w, out)
    r = run_bass_kernel_spmd(nc, [{f"in_{n}": a for n, a in arrays.items()}], core_ids=[0])
    return r.results[0]["out_x"]
```

```python
from contextlib import ExitStack

import concourse.bass as bass
import numpy as np
from concourse import mybir

F32 = mybir.dt.float32
BF16 = mybir.dt.bfloat16
I32 = mybir.dt.int32
ACT = mybir.ActivationFunctionType
ALU = mybir.AluOpType
AX = mybir.AxisListType

P = 128
B, T, C = 2, 2048, 256
HID = 1024
CH = C // P
CT = 256
NCHUNK = T // CT
W = B * CT
NQ = W // P
EPS = 1e-5
HEADS, DH = 16, 16
NPART = 3

VEC = ["attn_ln1_g", "attn_ln1_b", "attn_ln2_g", "attn_ln2_b", "time_decay", "time_first",
       "time_mix_k", "time_mix_v", "time_mix_r", "cm_k", "cm_r", "ffn_ln1_g", "ffn_ln1_b",
       "ffn_ln2_g", "ffn_ln2_b"]


def wait(eng, sem, count):
    if not (isinstance(count, int) and count <= 0):
        eng.wait_ge(sem, count)


def rwkv_phase(nc, x, vecs, w, out_scr):
    with ExitStack() as ctx:
        def sb(name, shape, dt=F32):
            return ctx.enter_context(nc.sbuf_tensor(name, shape, dt))

        def sem(name):
            return nc.alloc_semaphore(name)

        wk, wv, wr, wo = (sb(f"att_w{n}", [P, CH, C]) for n in "kvro")
        fr, qw, kw, vw = (sb(n, [P, CH, C]) for n in ("ffn_wr", "q_w", "k_w", "v_w"))
        fk = sb("ffn_wk", [P, CH, HID])
        fv = sb("ffn_wv", [P, HID // P, C])
        vec = sb("vec", [P, len(VEC), CH])
        omt = sb("one_minus_mix", [P, 5, CH])
        dec = sb("decay", [P, CH])
        decb = sb("decay_rows", [P, CH, CT])
        ident = sb("ident", [P, P])
        mhalf = sb("minus_half", [P, NQ])

        def col(name, d):
            n = VEC.index(name)
            return vec[:, n, d:d + 1]

        xin = sb("x_in", [P, NQ, C])
        h0 = [sb(f"x_norm{p}", [P, NQ, C]) for p in range(2)]
        st = sb("stats", [P, NQ, 6])
        mv = {n: sb(f"mean_var_{n}", [P, NQ, 2]) for n in ("0", "1", "2", "3", "4", "5")}
        rs = {n: sb(f"rstd_{n}", [P, NQ]) for n in mv}
        n1 = sb("n1", [P, NQ, C])
        xa = sb("xa", [P, CH, B, CT + 1])
        exps = sb("exps", [P, 4, CH, B, CT])
        mt = exps[:, 0:3]
        mx = sb("mixed", [P, 3, CH, B, CT])
        kk_, vv_, gate = (sb(n, [P, CH, B, CT]) for n in ("k", "v", "gate"))
        scan = sb("scan", [P, 3, CH, B, CT + 1])
        pp, aa, bb = (scan[:, n] for n in range(3))
        dd, ff = exps[:, 0:2], exps[:, 2:4]
        pm = sb("out_max", [P, CH, B, CT])
        ev = pm
        num = sb("num", [P, CH, B, CT])
        den = sb("den", [P, CH, B, CT])
        rw = sb("rwkv", [P, CH, B, CT])
        xres = sb("x_res", [P, NQ, C])
        x1 = sb("x1", [P, NQ, C])
        n2 = sb("n2", [P, NQ, C])
        xc = sb("xc", [P, CH, B, CT + 1])
        mx2 = sb("mixed2", [P, 2, CH, B, CT])
        rel = [sb(f"relu{p}", [P, W]) for p in range(2)]
        hid = sb("hidden", [P, HID // P, W])
        mt2 = hid[:, 0:4, :].rearrange("p (m d) (b t) -> p m d b t", m=2, b=B)
        sg = sb("sig", [P, NQ, C])
        x2 = sg
        X1, h1 = (sb(n + "_tile", [P, NQ, C]) for n in ("X1", "h1"))
        n3 = n2
        hT = mx2[:, 0].rearrange("p d b t -> p d (b t)")
        parts = sb("qk_parts", [P, 2, CH, NPART, W], BF16)
        rest = [sb(f"rest{p}", [P, W]) for p in range(2)]
        va = sb("v_aug", [P, NQ, HEADS, 2 * DH])

        psA = ctx.enter_context(nc.psum_tensor("psA", [P, 3, 512], F32))
        psB = ctx.enter_context(nc.psum_tensor("psB", [P, 5, 512], F32))
        tokB = psB[:, 0:2, :].rearrange("p a (q c) -> p (a q) c", c=C)
        tokR = psB[:, 2:4, :].rearrange("p a (q c) -> p (a q) c", c=C)

        s = {}

        def S(name):
            if name not in s:
                s[name] = sem("p1_" + name)
            return s[name]

        xr = x.rearrange("b (c h p) d -> c b p h d", h=CT // P, p=P)
        rows = {n: out_scr[n].rearrange("b (c h p) d -> c b p h d", h=CT // P, p=P) for n in ("X1", "h1")}
        var = out_scr["v_aug"].rearrange("b (c h) p n -> c b p h n", h=CT // P)
        pr = out_scr["parts"].rearrange("n r (d p) b (c t) -> n r c p d b t", p=P, t=CT)

        def tiles(b):
            return slice(b * NQ // B, (b + 1) * NQ // B)

        with nc.Block() as block:
            @block.sync
            def _(sp):
                def load_x(dst, i, name):
                    for b in range(B):
                        sp.dma_start(dst[:, tiles(b), :], xr[i, b]).then_inc(S(name), 16)

                load_x(xin, 0, "x_loaded")
                sp.dma_start(vec[:], vecs).then_inc(S("vec_loaded"), 16)
                for t, d in ((wk, "att_Wk"), (wv, "att_Wv"), (wr, "att_Wr")):
                    sp.dma_start(t[:], w[d].rearrange("(k p) n -> p k n", p=P)).then_inc(S("kvr_loaded"), 16)
                for t, d in ((wo, "att_Wo"), (fk, "ffn_Wk"),
                             (fv, "ffn_Wv"), (fr, "ffn_Wr"), (qw, "Wq"), (kw, "Wk"), (vw, "Wv")):
                    sp.dma_start(t[:], w[d].rearrange("(k p) n -> p k n", p=P)).then_inc(S("weights"), 16)
                load_x(xres, 0, "x_res_loaded")
                for i in (1, 2):
                    sp.wait_ge(S("x_read"), i)
                    load_x(xin, i, "x_loaded")

                def chunk(i):
                    if not (isinstance(i, int) and i >= NCHUNK - 3):
                        sp.wait_ge(S("x_read"), i + 3)
                        load_x(xin, i + 3, "x_loaded")
                    sp.wait_ge(S("X1"), i + 1)
                    for b in range(B):
                        sp.dma_start(rows["X1"][i, b], X1[:, tiles(b), :]).then_inc(S("X1_stored"), 16)
                    if not (isinstance(i, int) and i >= NCHUNK - 1):
                        load_x(xres, i + 1, "x_res_loaded")
                    sp.wait_ge(S("h1"), i + 1)
                    for b in range(B):
                        sp.dma_start(rows["h1"][i, b], h1[:, tiles(b), :]).then_inc(S("h1_stored"), 16)
                    sp.wait_ge(S("parts"), i + 1)
                    for n in range(2):
                        for r in range(NPART):
                            for d in range(CH):
                                sp.dma_start(pr[n, r, i, :, d], parts[:, n, d, r, :].rearrange(
                                    "p (b t) -> p b t", b=B)).then_inc(S("parts_stored"), 16)
                    sp.wait_ge(S("v_aug"), i + 1)
                    for b in range(B):
                        sp.dma_start(var[i, b], va[:, tiles(b)].rearrange("p h n m -> p h (n m)")).then_inc(
                            S("v_stored"), 16)

                chunk(0)
                with sp.Fori(1, NCHUNK - 3) as i:
                    chunk(i)
                for i in range(NCHUNK - 3, NCHUNK):
                    chunk(i)
                for n in ("X1", "h1", "v"):
                    sp.wait_ge(S(n + "_stored"), 16 * B * NCHUNK)
                sp.wait_ge(S("parts_stored"), 16 * NCHUNK * 2 * NPART * CH)

            def chunks(eng, step):
                step(-2, 0)
                step(-1, 1)
                step(0, 0)
                with eng.Fori(0, (NCHUNK - 4) // 2) as t:
                    step(2 * t + 1, 1)
                    step(2 * t + 2, 0)
                for i in range(NCHUNK - 3, NCHUNK):
                    step(i, i % 2)

            def exists(i):
                return not isinstance(i, int) or 0 <= i < NCHUNK

            @block.gpsimd
            def _(pool):
                pool.memset(ident[:], 0.0)
                pool.memset(mhalf[:], -0.5)
                pool.memset(xa[:], 0.0)
                pool.drain()
                pool.affine_select(out=ident[:], in_=ident[:], compare_op=ALU.not_equal, fill=1.0, base=0,
                                   pattern=[[-1, P]], channel_multiplier=1)
                pool.drain()
                pool.nop().then_inc(S("consts"), 1)

                def rstd(n, i):
                    if exists(i):
                        pool.wait_ge(S("stats" + n), i + 1)
                        pool.tensor_tensor(rs[n][:], rs[n][:], mhalf[:], ALU.pow).then_inc(S("rstd" + n), 1)

                def step(i, par):
                    rstd("0", i + 2)
                    rstd("1", i + 2)
                    if isinstance(i, int) and i == -2:
                        pool.memset(scan[:], 0.0)
                        pool.drain()
                        pool.memset(pp[:, :, :, CT:CT + 1], -1e38)
                        pool.drain()
                        pool.memset(xc[:], 0.0)
                        pool.memset(va[:], 1.0)
                        pool.drain()
                        pool.nop().then_inc(S("consts"), 1)
                    rstd("3", i)
                    rstd("4", i)
                    rstd("5", i)
                    rstd("2", i + 1)

                chunks(pool, step)

            @block.vector
            def _(v):
                def stats(n, src):
                    for q in range(NQ):
                        v.bn_stats(st[:, q, :], src[:, q, :])
                    v.drain()
                    for q in range(NQ):
                        v.bn_aggr(mv[n][:, q, :], st[:, q, :])
                    v.drain()
                    v.tensor_scalar(rs[n][:], mv[n][:, :, 1], EPS, None, ALU.add).then_inc(S("stats" + n), 1)

                def normalise(n, dst, src, i):
                    v.wait_ge(S("rstd" + n), i + 1)
                    for q in range(NQ):
                        ins = v.tensor_scalar(dst[:, q, :], src[:, q, :], mv[n][:, q, 0:1], rs[n][:, q:q + 1],
                                              ALU.subtract, ALU.mult)
                    return ins

                def layernorms(i, par):
                    v.wait_ge(S("x_loaded"), 32 * i + 32)
                    stats("0", xin)
                    normalise("0", h0[par], xin, i).then_inc(S("x_read"), 1)
                    v.drain()
                    stats("1", h0[par])
                    normalise("1", n1, h0[par], i).then_inc(S("n1"), 1)

                def mix(i):
                    v.wait_ge(S("mix_tmp"), i + 1)
                    for m, name in enumerate(("time_mix_k", "time_mix_v", "time_mix_r")):
                        for d in range(CH):
                            ins = v.scalar_tensor_tensor(mx[:, m, d], xa[:, d, :, 1:CT + 1], col(name, d),
                                                         mt[:, m, d], ALU.mult, ALU.add)
                    ins.then_inc(S("mixed"), 1)

                def wkv_exponents(i):
                    v.drain()
                    v.wait_ge(S("k"), i + 1)
                    v.tensor_copy(scan[:, :, :, :, 0], scan[:, :, :, :, CT])
                    v.drain()
                    for d in range(CH):
                        for b in range(B):
                            v.tensor_tensor_scan(pp[:, d, b, 1:], decb[:, d, :], kk_[:, d, b, :],
                                                 pp[:, d, b, 0:1], ALU.add, ALU.max)
                    v.drain()
                    for d in range(CH):
                        v.scalar_tensor_tensor(dd[:, 0, d], pp[:, d, :, 0:CT], dec[:, d:d + 1],
                                               pp[:, d, :, 1:], ALU.subtract, ALU.subtract)
                    v.tensor_tensor(dd[:, 1], kk_[:], pp[:, :, :, 1:], ALU.subtract).then_inc(S("dd"), 1)
                    for d in range(CH):
                        v.scalar_tensor_tensor(pm[:, d], kk_[:, d], col("time_first", d), pp[:, d, :, 0:CT],
                                               ALU.add, ALU.max)
                    v.drain()
                    for d in range(CH):
                        v.scalar_tensor_tensor(ff[:, 1, d], kk_[:, d], col("time_first", d), pm[:, d],
                                               ALU.add, ALU.subtract)
                    v.tensor_tensor(ff[:, 0], pp[:, :, :, 0:CT], pm[:], ALU.subtract).then_inc(S("ff"), 1)

                def mix2(i):
                    v.wait_ge(S("mix2_tmp"), i + 1)
                    for m, name in enumerate(("cm_k", "cm_r")):
                        for d in range(CH):
                            ins = v.scalar_tensor_tensor(mx2[:, m, d], xc[:, d, :, 1:CT + 1], col(name, d),
                                                         mt2[:, m, d], ALU.mult, ALU.add)
                    ins.then_inc(S("mixed2"), 1)

                def wkv_output(i):
                    v.drain()
                    v.wait_ge(S("v"), i + 1)
                    v.wait_ge(S("dd_exp"), i + 1)
                    v.tensor_tensor(ev[:], dd[:, 1], vv_[:], ALU.mult)
                    for d in range(CH):
                        for b in range(B):
                            v.tensor_tensor_scan(bb[:, d, b, 1:], dd[:, 0, d, b], dd[:, 1, d, b],
                                                 bb[:, d, b, 0:1], ALU.mult, ALU.add)
                    v.drain()
                    for d in range(CH):
                        for b in range(B):
                            v.tensor_tensor_scan(aa[:, d, b, 1:], dd[:, 0, d, b], ev[:, d, b],
                                                 aa[:, d, b, 0:1], ALU.mult, ALU.add)
                    v.drain()
                    v.wait_ge(S("ff_exp"), i + 1)
                    v.tensor_tensor(den[:], ff[:, 0], bb[:, :, :, 0:CT], ALU.mult)
                    v.drain()
                    v.tensor_tensor(num[:], ff[:, 0], aa[:, :, :, 0:CT], ALU.mult)
                    v.tensor_tensor(den[:], den[:], ff[:, 1], ALU.add)
                    v.drain()
                    v.tensor_tensor(ev[:], ff[:, 1], vv_[:], ALU.mult)
                    v.reciprocal(den[:], den[:])
                    v.drain()
                    v.tensor_tensor(num[:], num[:], ev[:], ALU.add)
                    v.wait_ge(S("gate"), i + 1)
                    v.tensor_tensor(den[:], den[:], gate[:], ALU.mult)
                    v.drain()
                    v.tensor_tensor(rw[:], num[:], den[:], ALU.mult).then_inc(S("rw"), 1)

                def channel_mix_out(i):
                    v.wait_ge(S("sig"), i + 1)
                    v.wait_ge(S("kv"), i + 1)
                    v.tensor_tensor(x2[:], sg[:], tokB, ALU.mult).then_inc(S("kv_read"), 1)
                    v.drain()
                    v.tensor_tensor(x2[:], x2[:], x1[:], ALU.add)
                    v.drain()
                    stats("3", x2)
                    normalise("3", x2, x2, i)

                def outer_residual(i):
                    v.drain()
                    v.wait_ge(S("x_res_loaded"), 32 * i + 32)
                    wait(v, S("X1_stored"), 32 * i)
                    v.tensor_tensor(X1[:], x2[:], xres[:], ALU.add).then_inc(S("X1"), 1)
                    v.drain()
                    stats("4", X1)
                    wait(v, S("h1_stored"), 32 * i)
                    normalise("4", h1, X1, i).then_inc(S("h1"), 1)
                    v.drain()
                    stats("5", h1)
                    normalise("5", n3, h1, i).then_inc(S("n3"), 1)

                def time_mix_residual(i, par):
                    v.drain()
                    v.wait_ge(S("att_out"), i + 1)
                    v.tensor_tensor(x1[:], tokB, h0[par][:], ALU.add).then_inc(S("x1"), 1)
                    v.drain()
                    stats("2", x1)

                def split(i, m):
                    n, d = m // 2, m % 2
                    v.wait_ge(S("part0"), 4 * i + m + 1)
                    v.tensor_tensor(rest[m % 2][:], psB[:, 2 + m % 3, :], parts[:, n, d, 0, :],
                                    ALU.subtract).then_inc(S("rest"), 1)
                    v.wait_ge(S("part1"), 4 * i + m + 1)
                    return v.tensor_tensor(parts[:, n, d, 2, :], rest[m % 2][:], parts[:, n, d, 1, :],
                                           ALU.subtract)

                def step(i, par):
                    if exists(i + 1):
                        wkv_exponents(i + 1)
                    if exists(i):
                        mix2(i)
                    if exists(i + 1):
                        wkv_output(i + 1)
                    if exists(i + 2):
                        layernorms(i + 2, par)
                        if isinstance(i, int) and i == -2:
                            constants()
                    if exists(i):
                        channel_mix_out(i)
                    if exists(i + 2):
                        mix(i + 2)
                    if exists(i):
                        outer_residual(i)
                    if exists(i + 1):
                        time_mix_residual(i + 1, 1 - par)
                    if exists(i):
                        split(i, 0)
                        split(i, 1)
                    if exists(i + 1):
                        normalise("2", n2, x1, i + 1).then_inc(S("n2"), 1)
                    if exists(i):
                        split(i, 2)
                        split(i, 3).then_inc(S("parts"), 1)

                def constants():
                    v.wait_ge(S("vec_loaded"), 16)
                    for n, name in enumerate(("time_mix_k", "time_mix_v", "time_mix_r", "cm_k", "cm_r")):
                        ins = v.tensor_scalar(omt[:, n, :], vec[:, VEC.index(name), :], -1.0, 1.0, ALU.mult, ALU.add)
                    ins.then_inc(S("omt"), 1)
                    v.memset(decb[:], 0.0)
                    v.wait_ge(S("decay"), 1)
                    v.drain()
                    for d in range(CH):
                        v.tensor_scalar(decb[:, d, :], decb[:, d, :], dec[:, d:d + 1], None, ALU.subtract)
                    v.drain()
                    v.wait_ge(S("consts"), 2)

                chunks(v, step)

            @block.scalar
            def _(act):
                act.wait_ge(S("vec_loaded"), 16)
                act.activation(dec[:], vec[:, VEC.index("time_decay"), :], ACT.Exp).then_inc(S("decay"), 1)
                act.wait_ge(S("consts"), 2)

                def transposed(dst, g, b, src, i, name, bank):
                    act.wait_ge(S(name), i + 1)
                    act.copy(dst[:, :, :, 0], dst[:, :, :, CT])
                    act.drain()
                    for d in range(CH):
                        act.activation(dst[:, d, :, 1:], src[:, bank + d, :].rearrange("p (b t) -> p b t", b=B),
                                       ACT.Identity, scale=col(g, d), bias=col(b, d))
                    act.drain()

                def mix2_tmp(i):
                    transposed(xc, "attn_ln2_g", "attn_ln2_b", psB, i, "n2T", 2)
                    for m in range(2):
                        for d in range(CH):
                            ins = act.activation(mt2[:, m, d], xc[:, d, :, 0:CT], ACT.Copy,
                                                 scale=omt[:, 3 + m, d:d + 1])
                    ins.then_inc(S("mix2_tmp"), 1)

                def exponentials(i):
                    act.wait_ge(S("dd"), i + 1)
                    act.activation(dd[:], dd[:], ACT.Exp).then_inc(S("dd_exp"), 1)
                    act.wait_ge(S("ff"), i + 1)
                    act.activation(ff[:], ff[:], ACT.Exp).then_inc(S("ff_exp"), 1)

                def hidden(i):
                    for h in range(HID // P):
                        act.wait_ge(S("hid_psum"), 8 * i + h + 1)
                        act.activation(rel[h % 2][:], psB[:, 2 + h % 3, :], ACT.Relu).then_inc(S("relu"), 1)
                        act.drain()
                        act.activation(hid[:, h, :], rel[h % 2][:], ACT.Square).then_inc(S("hid"), 1)
                    act.wait_ge(S("r2"), i + 1)
                    act.activation(sg[:], tokR, ACT.Sigmoid).then_inc(S("sig"), 1)

                def mix_tmp(i):
                    transposed(xa, "attn_ln1_g", "attn_ln1_b", psA, i, "n1T", 0)
                    wait(act, S("rw"), i)
                    for m in range(3):
                        for d in range(CH):
                            ins = act.activation(mt[:, m, d], xa[:, d, :, 0:CT], ACT.Copy, scale=omt[:, m, d:d + 1])
                    ins.then_inc(S("mix_tmp"), 1)

                def projections(i):
                    for m, (dst, name) in enumerate(((kk_, "k"), (vv_, "v"), (gate, "gate"))):
                        for d in range(CH):
                            act.wait_ge(S("proj"), 6 * i + 2 * m + d + 1)
                            act.activation(dst[:, d].rearrange("p b t -> p (b t)"), psA[:, (2 * m + d) % 3, :],
                                           ACT.Sigmoid if m == 2 else ACT.Copy).then_inc(S("proj_read"), 1)
                        act.drain()
                        act.nop().then_inc(S(name), 1)

                def qkv(i):
                    act.wait_ge(S("n3T"), i + 1)
                    for d in range(CH):
                        ins = act.activation(hT[:, d, :], psB[:, 2 + d, :], ACT.Identity,
                                             scale=col("ffn_ln1_g", d), bias=col("ffn_ln1_b", d))
                    ins.then_inc(S("hT"), 1)
                    wait(act, S("parts_stored"), 16 * 12 * i)
                    for m in range(4):
                        n, d = m // 2, m % 2
                        act.wait_ge(S("qk"), 4 * i + m + 1)
                        act.activation(parts[:, n, d, 0, :], psB[:, 2 + m % 3, :], ACT.Copy).then_inc(
                            S("part0"), 1)
                        act.wait_ge(S("rest"), 4 * i + m + 1)
                        act.activation(parts[:, n, d, 1, :], rest[m % 2][:], ACT.Copy).then_inc(S("part1"), 1)
                    wait(act, S("v_stored"), 32 * i)
                    act.wait_ge(S("v_psum"), i + 1)
                    act.activation(va[:, :, :, 0:DH], tokB.rearrange("p q (n m) -> p q n m", m=DH),
                                   ACT.Copy).then_inc(S("v_aug"), 1)

                def step(i, par):
                    if exists(i):
                        mix2_tmp(i)
                    if exists(i + 1):
                        exponentials(i + 1)
                    if exists(i):
                        hidden(i)
                    if exists(i + 2):
                        mix_tmp(i + 2)
                        projections(i + 2)
                    if exists(i):
                        qkv(i)

                act.wait_ge(S("omt"), 1)
                chunks(act, step)

            @block.tensor
            def _(pe):
                pe.wait_ge(S("consts"), 1)

                def transposes(ps, bank, src):
                    for q in range(NQ):
                        for d in range(CH):
                            ins = pe.transpose(ps[:, bank + d, q * P:(q + 1) * P], src[:, q, d * P:(d + 1) * P],
                                               ident[:])
                    return ins

                def tokens(dst, lhs, rhs, n):
                    for q in range(NQ):
                        for k in range(n):
                            ins = pe.matmul(dst[:, q, :], lhs(k, q), rhs[:, k, :], start=(k == 0), stop=(k == n - 1))
                    return ins

                def channel_mix(i):
                    pe.wait_ge(S("n2"), i + 1)
                    wait(pe, S("rest"), 4 * i)
                    transposes(psB, 2, n2).then_inc(S("n2T"), 1)
                    pe.wait_ge(S("mixed2"), i + 1)
                    for h in range(HID // P):
                        if h >= 3:
                            pe.wait_ge(S("relu"), 8 * i + h - 2)
                        for d in range(CH):
                            ins = pe.matmul(psB[:, 2 + h % 3, :], fk[:, d, h * P:(h + 1) * P],
                                            mx2[:, 0, d].rearrange("p b t -> p (b t)"),
                                            start=(d == 0), stop=(d == CH - 1))
                        ins.then_inc(S("hid_psum"), 1)
                    pe.wait_ge(S("relu"), 8 * i + 8)
                    fl = mx2.rearrange("p m d b t -> p m d (b t)")
                    tokens(tokR, lambda k, q: fl[:, 1, k, q * P:(q + 1) * P], fr, CH).then_inc(S("r2"), 1)
                    pe.wait_ge(S("hid"), 8 * i + 8)
                    wait(pe, S("v_aug"), i)
                    tokens(tokB, lambda k, q: hid[:, k, q * P:(q + 1) * P], fv, HID // P).then_inc(S("kv"), 1)

                def projections(i):
                    pe.wait_ge(S("n1"), i + 1)
                    wait(pe, S("proj_read"), 6 * i)
                    transposes(psA, 0, n1).then_inc(S("n1T"), 1)
                    pe.wait_ge(S("mixed"), i + 1)
                    for m, wt in enumerate((wk, wv, wr)):
                        for o in range(CH):
                            j = 2 * m + o
                            if j >= 3:
                                pe.wait_ge(S("proj_read"), 6 * i + j - 2)
                            for d in range(CH):
                                ins = pe.matmul(psA[:, j % 3, :], wt[:, d, o * P:(o + 1) * P],
                                                mx[:, m, d].rearrange("p b t -> p (b t)"),
                                                start=(d == 0), stop=(d == CH - 1))
                            ins.then_inc(S("proj"), 1)

                def attention_out(i):
                    wait(pe, S("kv_read"), i)
                    pe.wait_ge(S("rw"), i + 1)
                    flat = rw.rearrange("p d b t -> p d (b t)")
                    tokens(tokB, lambda k, q: flat[:, k, q * P:(q + 1) * P], wo, CH).then_inc(S("att_out"), 1)

                def qkv(i, last):
                    pe.wait_ge(S("n3"), i + 1)
                    pe.wait_ge(S("sig"), i + 1)
                    transposes(psB, 2, n3).then_inc(S("n3T"), 1)
                    pe.wait_ge(S("hT"), i + 1)
                    for m in range(4):
                        wt, o = (qw, kw)[m // 2], m % 2
                        if m == 3:
                            pe.wait_ge(S("rest"), 4 * i + 1)
                        for d in range(CH):
                            ins = pe.matmul(psB[:, 2 + m % 3, :], wt[:, d, o * P:(o + 1) * P], hT[:, d, :],
                                            start=(d == 0), stop=(d == CH - 1))
                        ins.then_inc(S("qk"), 1)
                    if last:
                        pe.wait_ge(S("kv_read"), i + 1)
                    else:
                        pe.wait_ge(S("x1"), i + 2)
                    tokens(tokB, lambda k, q: hT[:, k, q * P:(q + 1) * P], vw, CH).then_inc(S("v_psum"), 1)

                def step(i, par):
                    if isinstance(i, int) and i == -2:
                        pe.wait_ge(S("kvr_loaded"), 16 * 3)
                    if exists(i):
                        channel_mix(i)
                    if exists(i + 2):
                        projections(i + 2)
                    if isinstance(i, int) and i == -1:
                        pe.wait_ge(S("weights"), 16 * 7)
                    if exists(i + 1):
                        attention_out(i + 1)
                    if exists(i):
                        qkv(i, not exists(i + 1))

                chunks(pe, step)

        nc.clear_and_free_semaphores(list(s.values()))
        nc.all_engine_barrier()


GROUPS = HEADS // 4
UNITS = B * GROUPS
QW = 512
NWIN = UNITS * (T // QW)
KT = T // P
KPARTS = (0, 1, 2, 0, 1, 0)
QPARTS = (0, 0, 0, 1, 1, 2)
ROWS = DH * len(KPARTS)
AHEAD = 4


def attention_phase(nc, scr, beside):
    with ExitStack() as ctx:
        def sb(name, shape, dt=F32):
            return ctx.enter_context(nc.sbuf_tensor(name, shape, dt))

        kst = sb("k_stack", [P, 2, 4, T], BF16)
        qst = sb("q_stack", [P, 2, T // QW, 4, QW], BF16)
        vt = sb("v_tiles", [P, KT, P])
        pb = [sb(f"probs{p}", [P, 4, QW]) for p in range(2)]
        pmx = sb("part_max", [P, 16, 4])
        nmf = sb("neg_max", [P, 16])
        nmr = sb("neg_max_rest", [P, 16])
        nm3 = sb("neg_max_parts", [P, P // 16, 16], BF16)
        nmT = sb("neg_max_rows", [NPART * 16, P], BF16)
        csb = sb("ctx_sums", [P, QW])
        idb = sb("ident_bf", [P, P], BF16)

        psS = ctx.enter_context(nc.psum_tensor("ps_scores_t", [P, 4, QW], F32))
        psM = ctx.enter_context(nc.psum_tensor("ps_scores", [P, 3, QW], F32))
        psC = ctx.enter_context(nc.psum_tensor("ps_ctx", [P, QW], F32))
        BANK = (0, 2, 1, 2)
        psT = psM[:, 1, :].bitcast(BF16)
        s = {}

        def S(name):
            if name not in s:
                s[name] = nc.alloc_semaphore("p2_" + name)
            return s[name]

        src = scr["parts"].rearrange("n r (g h d) b t -> n r b g d h t", g=GROUPS, h=4)
        vsrc = scr["v_aug"].rearrange("b (c k) p (g n) -> b g c p k n", c=4, g=GROUPS)
        cdst = scr["ctx"]
        NLOAD = 5 * len(KPARTS)

        with nc.Block() as block:
            @block.sync
            def _(sp):
                def load_qk(b, g, par):
                    for blk in range(len(KPARTS)):
                        r = slice(DH * blk, DH * blk + DH)
                        sp.dma_start(kst[r, par], src[1, KPARTS[blk], b, g]).then_inc(S("qk_loaded"), 16)
                        for h in range(4):
                            sp.dma_start(qst[r, par, :, h, :], src[0, QPARTS[blk], b, g, :, h].rearrange(
                                "d (c t) -> d c t", t=QW)).then_inc(S("qk_loaded"), 16)

                def load_v(b, g, c):
                    sp.dma_start(vt[:, 4 * c:4 * c + 4, :], vsrc[b, g, c]).then_inc(S(f"v_loaded{c}"), 16)

                def neg_max(w, qc, par):
                    sp.wait_ge(S("nmT"), w + 1)
                    for r in range(NPART):
                        sp.dma_start(qst[ROWS + r:ROWS + r + 1, par, qc].rearrange("a h t -> a (h t)").rearrange("a (n t) -> a n t", t=P),
                                     nmT[16 * r:16 * r + 16, :]).then_inc(S("neg_max"), 16)

                def unit(b, g, u, par, nxt):
                    if nxt:
                        if not isinstance(u, int) or u > 0:
                            sp.wait_ge(S("pv"), 2 + 64 * u)
                        load_qk(*nxt, 1 - par)
                    for qc in range(3):
                        neg_max(4 * u + qc + 1, qc + 1, par)
                    if nxt:
                        for c in range(4):
                            if c == 3:
                                neg_max(4 * u + 4, 0, 1 - par)
                            sp.wait_ge(S("pv"), 2 + 64 * u + 48 + 4 * c + 4)
                            load_v(*nxt, c)

                load_qk(0, 0, 0)
                for c in range(4):
                    load_v(0, 0, c)
                sp.wait_ge(S("ones"), 1)
                beside.start(sp)
                neg_max(0, 0, 0)
                unit(0, 0, 0, 0, (0, 1))
                unit(0, 1, 1, 1, (0, 2))
                unit(0, 2, 2, 0, (0, 3))
                unit(0, 3, 3, 1, (1, 0))
                unit(1, 0, 4, 0, (1, 1))
                unit(1, 1, 5, 1, (1, 2))
                unit(1, 2, 6, 0, (1, 3))
                unit(1, 3, 7, 1, None)
                beside.finish(sp)

            def windows(eng, window):
                window(0, first=True)
                with eng.Fori(1, NWIN - 2) as w:
                    window(w)
                window(NWIN - 2, left=1)
                window(NWIN - 1, left=0)

            def job_of(w, kt, left):
                if kt < 16 - AHEAD:
                    return (w + 1, kt + AHEAD) if left > 0 else None
                return (w + 2, kt - 16 + AHEAD) if left > 1 else None

            @block.tensor
            def _(pe):
                pe.nop().then_inc(S("pv"), 2)
                pe.wait_ge(S("ones"), 1)
                pe.wait_ge(S("exp"), 2)
                pe.wait_ge(S("max_read"), 4)

                def job(mn, c):
                    if mn is None:
                        return
                    m, n = mn
                    h, q = n // 4, n % 4
                    par, qc = (m // 4) % 2, m % 4
                    if c == 0 and n == 0:
                        pe.wait_ge(S("qk_loaded"), 16 * NLOAD * (m // 4) + 16 * NLOAD)
                    pe.wait_ge(S("max_read"), 64 * m + 4 * n + (1, 4, 3, 6)[c])
                    pe.matmul(psM[:, BANK[c], :], qst[0:ROWS, par, qc, h, q * P:(q + 1) * P],
                              kst[0:ROWS, par, h, c * QW:(c + 1) * QW], start=True, stop=True).then_inc(
                        S("max_scores"), 1)

                def scores(w, kt, p):
                    par, qc = (w // 4) % 2, w % 4
                    pe.wait_ge(S("exp"), 32 * w + 2 * kt + p + 1)
                    for h in range(2 * p, 2 * p + 2):
                        ins = pe.matmul(psS[:, h, :], kst[0:ROWS + NPART, par, h, kt * P:(kt + 1) * P],
                                        qst[0:ROWS + NPART, par, qc, h, :], start=True, stop=True)
                    ins.then_inc(S("scores"), 1)

                def values(w, kt):
                    if kt % 4 == 0:
                        pe.wait_ge(S(f"v_loaded{kt // 4}"), 16 * (w // 4) + 16)
                    if kt == 0:
                        wait(pe, S("ctx_read"), w)
                    pe.wait_ge(S("exp"), 32 * w + 2 * kt + 4)
                    for h in range(4):
                        ins = pe.matmul(psC[32 * h:32 * h + 32, :], vt[:, kt, 32 * h:32 * h + 32],
                                        pb[kt % 2][:, h, :], start=(kt == 0), stop=(kt == KT - 1))
                    ins.then_inc(S("pv"), 1)

                def turn_max(m):
                    pe.wait_ge(S("neg_max_parts"), m + 1)
                    pe.transpose(psT[:, 0:P], nm3.rearrange("p r n -> p (r n)"), idb[:]).then_inc(
                        S("neg_max_turned"), 1)

                for n in range(16 + AHEAD):
                    for c in range(4):
                        if (n, c) == (16, 2):
                            turn_max(0)
                            pe.wait_ge(S("nmT"), 1)
                        job((n // 16, n % 16), c)

                def window(w, first=False, left=2):
                    pe.wait_ge(S("neg_max"), 48 * w + 48)
                    for kt in range(KT):
                        mn = job_of(w, kt, left)
                        scores(w, kt, 0)
                        job(mn, 0)
                        scores(w, kt, 1)
                        job(mn, 1)
                        turn = kt == 16 - AHEAD and left
                        if turn:
                            turn_max(w + 1)
                        else:
                            job(mn, 2)
                        if kt > 0:
                            values(w, kt - 1)
                        elif not first:
                            values(w - 1, KT - 1)
                        if turn:
                            pe.wait_ge(S("nmT"), w + 2)
                            job(mn, 2)
                        job(mn, 3)

                windows(pe, window)
                values(NWIN - 1, KT - 1)

            @block.scalar
            def _(act):
                act.nop().then_inc(S("exp"), 2)

                def context(w):
                    act.wait_ge(S("sums_free"), w + 1)
                    act.wait_ge(S("pv"), 2 + 16 * w + 16)
                    act.copy(csb[:], psC[:]).then_inc(S("ctx_read"), 1)

                def window(w, first=False, left=2):
                    for kt in range(KT):
                        act.wait_ge(S("pv"), 16 * w + kt + 1)
                        for p in range(2):
                            act.wait_ge(S("scores"), 32 * w + 2 * kt + p + 1)
                            act.activation(pb[kt % 2][:, 2 * p:2 * p + 2, :], psS[:, 2 * p:2 * p + 2, :], ACT.Exp,
                                           scale=DH ** -0.5).then_inc(S("exp"), 1)
                        if kt == 0 and not first:
                            context(w - 1)

                windows(act, window)
                context(NWIN - 1)

            @block.vector
            def _(v):
                v.nop().then_inc(S("max_read"), 4)
                v.wait_ge(S("ones"), 1)

                def job(m, n, rows_of=None):
                    for c in range(4):
                        if c == 2 and rows_of is not None:
                            neg_max_rows(rows_of)
                        v.wait_ge(S("max_scores"), 64 * m + 4 * n + c + 1)
                        v.tensor_reduce(pmx[:, n, c:c + 1], psM[:, BANK[c], :], AX.X, ALU.max).then_inc(
                            S("max_read"), 1)

                def neg_max(m):
                    v.wait_ge(S("max_read"), 64 * m + 68)
                    v.tensor_reduce(nmf[:], pmx[:], AX.X, ALU.max, negate=True)
                    v.drain()
                    v.tensor_copy(nm3[:, 0, :], nmf[:])
                    v.drain()
                    v.tensor_tensor(nmr[:], nmf[:], nm3[:, 0, :], ALU.subtract)
                    v.drain()
                    v.tensor_copy(nm3[:, 1, :], nmr[:])
                    v.drain()
                    v.tensor_tensor(nm3[:, 2, :], nmr[:], nm3[:, 1, :], ALU.subtract).then_inc(
                        S("neg_max_parts"), 1)

                def neg_max_rows(m):
                    wait(v, S("neg_max"), 48 * m)
                    v.wait_ge(S("neg_max_turned"), m + 1)
                    v.tensor_copy(nmT[:], psT[0:NPART * 16, 0:P]).then_inc(S("nmT"), 1)

                for n in range(16 + AHEAD):
                    job(n // 16, n % 16, rows_of=0 if n == 16 else None)
                    if n == 15:
                        neg_max(0)

                def window(w, first=False, left=2):
                    for kt in range(KT):
                        mn = job_of(w, kt, left)
                        turn = kt == 16 - AHEAD and left
                        if mn:
                            job(*mn, rows_of=w + 1 if turn else None)
                        elif turn:
                            neg_max_rows(w + 1)
                        if kt == 15 - AHEAD and left:
                            neg_max(w + 1)

                windows(v, window)

            @block.gpsimd
            def _(pool):
                pool.memset(kst[ROWS:ROWS + 32], 1.0)
                pool.drain()
                beside.clear(pool)
                pool.drain()
                pool.memset(nm3[:], 0.0)
                pool.drain()
                pool.memset(idb[:], 0.0)
                pool.drain()
                pool.affine_select(out=idb[:], in_=idb[:], compare_op=ALU.not_equal, fill=1.0, base=0,
                                   pattern=[[-1, P]], channel_multiplier=1)
                pool.drain()
                pool.nop().then_inc(S("ones"), 1)
                pool.nop().then_inc(S("sums_free"), 1)
                with pool.Fori(0, NWIN) as w:
                    pool.wait_ge(S("ctx_read"), w + 1)
                    pool.dma_start(cdst[w], csb[:]).then_inc(S("ctx_stored"), 16)
                    pool.wait_ge(S("ctx_stored"), 16 * w + 16)
                    pool.nop().then_inc(S("sums_free"), 1)


E_ = 8
F = 1024
TB = T // P
N = B * TB
NT = 2 * N + E_ - 1


def route_phase(nc, w, vec, scr, xn, slot, wts, eid):
    with ExitStack() as ctx:
        def sb(name, shape, dt=F32):
            return ctx.enter_context(nc.sbuf_tensor(f"r_{name}", shape, dt))

        s = {}

        def S(name):
            if name not in s:
                s[name] = nc.alloc_semaphore(f"r_{name}")
            return s[name]

        wo = sb("wo", [P, GROUPS, C])
        wg = sb("wg", [P, CH, E_])
        ident = sb("ident", [P, P])
        ones = sb("ones", [P, P])
        below = sb("below", [P, P])
        mhalf = sb("minus_half", [P, NQ])
        iota_i = sb("iota_i", [P, NT], I32)
        iota = sb("iota", [P, NT])
        rsum = sb("row_sums", [NWIN * 4, QW])
        rbc = [sb(f"inv_sums{b}", [P, GROUPS, QW]) for b in range(B)]
        cx = [sb(f"ctx{b}", [P, GROUPS, QW]) for b in range(B)]
        xm = [sb(f"x_mid{b}", [P, NQ, C]) for b in range(B)]
        st = [sb(f"stats{b}", [P, NQ, 6]) for b in range(B)]
        mv = [sb(f"mean_var{b}", [P, NQ, 2]) for b in range(B)]
        rs = [sb(f"rstd{b}", [P, NQ]) for b in range(B)]
        n_tile = [sb(f"n_tile{b}", [P, NQ, C]) for b in range(B)]
        mT = sb("mT", [P, CH, W])
        lg = sb("logits", [P, N, E_])
        t8 = sb("top8", [P, N, E_])
        i8 = sb("top8_idx", [P, N, E_], mybir.dt.uint32)
        fi = sb("idx_f", [P, N, E_])
        c1 = sb("choice", [P, N])
        m12 = sb("one_hot", [P, 2, N, E_])
        cnt = sb("count", [P, N, E_])
        te = sb("tiles_of_expert", [P, E_])
        tc = sb("tiles_cum", [P, E_])
        zero = sb("zero", [P, N])
        off = sb("start", [P, E_])
        sf = sb("slot_f", [P, N])
        free = rbc[0].rearrange("p g t -> p (g t)")
        tot, cum, tmp = (free[:, N * E_ * k:N * E_ * (k + 1)].rearrange("p (n e) -> p n e", e=E_) for k in range(3))
        tl = free[:, N * E_ * 3:N * E_ * 4].rearrange("p (e n) -> p e n", e=E_)
        ee = free[:, N * E_ * 4:N * E_ * 4 + NT * (E_ - 1)].rearrange("p (n e) -> p n e", e=E_ - 1)
        ef = sb("expert_f", [P, NT])
        ps = ctx.enter_context(nc.psum_tensor("r_ps", [P, 8, 512], F32))
        tok = [ps[:, 2 * b:2 * b + 2, :].rearrange("p a (q c) -> p (a q) c", c=C) for b in range(B)]
        psl = [ps[:, 6 + b, 0:NQ * E_].rearrange("p (n e) -> p n e", e=E_) for b in range(B)]
        psc = ps[:, 7, 0:2 * N * E_].rearrange("p (k n e) -> p k n e", k=2, e=E_)

        sums = scr["ctx"].rearrange("w (h r) t -> (w h) r t", h=4)[:, DH, :]
        inv = scr["inv"].rearrange("(b g c h) t -> b c h g t", b=B, g=GROUPS, h=4)
        cin = scr["ctx"].rearrange("(b g c) p t -> b c p g t", b=B, g=GROUPS)
        hin = scr["h1"].rearrange("b (c q p) d -> b c p q d", q=NQ, p=P)
        xout = scr["x_mid"].rearrange("b (c q p) d -> b c p q d", q=NQ, p=P)
        NC = T // W

        with nc.Block() as block:
            @block.sync
            def _(sp):
                def load_ctx(b, c):
                    sp.dma_start(cx[b][:], cin[b, c]).then_inc(S(f"ctx{b}"), 16)
                    for j in range(4):
                        sp.dma_start(rbc[b][32 * j:32 * j + 32], inv[b, c, j].partition_broadcast(32)).then_inc(
                            S(f"ctx{b}"), 16)

                def load_h1(b, c):
                    sp.dma_start(xm[b][:], hin[b, c]).then_inc(S(f"h1{b}"), 16)

                sp.dma_start(rsum[:], sums).then_inc(S("sums"), 16)
                for b in range(B):
                    load_h1(b, 0)
                sp.wait_ge(S("zeroed"), 1)
                for j in range(4):
                    sp.dma_start(wo[32 * j:32 * j + DH], w["Wo"].rearrange("(g j d) n -> j d g n", j=4, d=DH)[j]
                                 ).then_inc(S("weights"), 16)
                sp.dma_start(wg[:], w["Wg"].rearrange("(k p) n -> p k n", p=P)).then_inc(S("weights"), 16)
                sp.wait_ge(S("inv"), 1)
                sp.dma_start(scr["inv"], rsum[:]).then_inc(S("inv_stored"), 16)
                sp.wait_ge(S("inv_stored"), 16)
                for b in range(B):
                    load_ctx(b, 0)

                def chunk(c, last):
                    if not last:
                        for b in range(B):
                            sp.wait_ge(S("proj"), B * c + b + 1)
                            load_ctx(b, c + 1)
                    for b in range(B):
                        sp.wait_ge(S("x_mid"), B * c + b + 1)
                        sp.dma_start(xout[b, c], xm[b][:]).then_inc(S(f"x_stored{b}"), 16)
                    if not last:
                        for b in range(B):
                            sp.wait_ge(S("norm"), B * c + b + 1)
                            sp.wait_ge(S(f"x_stored{b}"), 16 * c + 16)
                            load_h1(b, c + 1)

                with sp.Fori(0, NC - 1) as c:
                    chunk(c, False)
                chunk(NC - 1, True)
                for b in range(B):
                    sp.wait_ge(S(f"x_stored{b}"), 16 * NC)

            @block.gpsimd
            def _(pool):
                pool.memset(wo[:], 0.0)
                pool.drain()
                pool.nop().then_inc(S("zeroed"), 1)
                pool.memset(ident[:], 0.0)
                pool.memset(ones[:], 1.0)
                pool.memset(mhalf[:], -0.5)
                pool.iota(iota_i[:], [[1, NT]], base=0, channel_multiplier=0)
                pool.drain()
                pool.affine_select(out=ident[:], in_=ident[:], compare_op=ALU.not_equal, fill=1.0, base=0,
                                   pattern=[[-1, P]], channel_multiplier=1)
                pool.affine_select(out=below[:], in_=ones[:], compare_op=ALU.is_gt, fill=0.0, base=0,
                                   pattern=[[1, P]], channel_multiplier=-1)
                pool.drain()
                pool.nop().then_inc(S("consts"), 1)
                with pool.Fori(0, NC) as c:
                    for b in range(B):
                        pool.wait_ge(S("stats"), B * c + b + 1)
                        pool.tensor_tensor(rs[b][:], rs[b][:], mhalf[:], ALU.pow).then_inc(S("rstd"), 1)

            @block.tensor
            def _(pe):
                pe.wait_ge(S("weights"), 16 * 5)
                pe.wait_ge(S("consts"), 1)
                with pe.Fori(0, NC) as c:
                    for b in range(B):
                        pe.wait_ge(S("scaled"), B * c + b + 1)
                        for q in range(NQ):
                            for g in range(GROUPS):
                                ins = pe.matmul(tok[b][:, q, :], cx[b][:, g, q * P:(q + 1) * P], wo[:, g, :],
                                                start=(g == 0), stop=(g == GROUPS - 1))
                        ins.then_inc(S("proj"), 1)
                    for b in range(B):
                        pe.wait_ge(S("norm"), B * c + b + 1)
                        for q in range(NQ):
                            for d in range(CH):
                                ins = pe.transpose(ps[:, 4 + d, q * P:(q + 1) * P],
                                                   n_tile[b][:, q, d * P:(d + 1) * P], ident[:])
                        ins.then_inc(S("turned"), 1)
                        pe.wait_ge(S("mT"), B * c + b + 1)
                        for q in range(NQ):
                            for d in range(CH):
                                ins = pe.matmul(psl[b][:, q, :], mT[:, d, q * P:(q + 1) * P], wg[:, d, :],
                                                start=(d == 0), stop=(d == CH - 1))
                        ins.then_inc(S("logits"), 1)
                pe.wait_ge(S("count"), 1)
                flat = cnt.rearrange("p n e -> p (n e)")
                for k, m in enumerate((below, ones)):
                    ins = pe.matmul(ps[:, 7, k * N * E_:(k + 1) * N * E_], m[:], flat, start=True, stop=True)
                ins.then_inc(S("prefix"), 1)

            @block.scalar
            def _(act):
                with act.Fori(0, NC) as c:
                    for b in range(B):
                        act.wait_ge(S("norm"), B * c + b + 1)
                        act.copy(xn[:, bass.ds(NQ * c + TB * b, NQ), :], n_tile[b][:])
                        act.wait_ge(S("turned"), B * c + b + 1)
                        for d in range(CH):
                            ins = act.activation(mT[:, d, :], ps[:, 4 + d, :], ACT.Identity,
                                                 scale=vec[:, VEC.index("ffn_ln2_g"), d:d + 1],
                                                 bias=vec[:, VEC.index("ffn_ln2_b"), d:d + 1])
                        ins.then_inc(S("mT"), 1)
                act.wait_ge(S("shifted"), 1)
                act.activation(lg[:], lg[:], ACT.Exp).then_inc(S("exp"), 1)

            @block.vector
            def _(v):
                v.wait_ge(S("sums"), 16)
                v.reciprocal(rsum[:], rsum[:]).then_inc(S("inv"), 1)
                v.memset(zero[:], 0.0)
                v.wait_ge(S("consts"), 1)
                v.tensor_copy(iota[:], iota_i[:])

                def scale(c):
                    for b in range(B):
                        v.wait_ge(S(f"ctx{b}"), 80 * c + 80)
                        v.tensor_tensor(cx[b][:], cx[b][:], rbc[b][:], ALU.mult).then_inc(S("scaled"), 1)

                def chunk(c, last):
                    for b in range(B):
                        v.wait_ge(S(f"h1{b}"), 16 * c + 16)
                        v.wait_ge(S("proj"), B * c + b + 1)
                        v.tensor_tensor(xm[b][:], tok[b], xm[b][:], ALU.add).then_inc(S("x_mid"), 1)
                        v.drain()
                        for q in range(NQ):
                            v.bn_stats(st[b][:, q, :], xm[b][:, q, :])
                        v.drain()
                        for q in range(NQ):
                            v.bn_aggr(mv[b][:, q, :], st[b][:, q, :])
                        v.drain()
                        v.tensor_scalar(rs[b][:], mv[b][:, :, 1], EPS, None, ALU.add).then_inc(S("stats"), 1)
                    for b in range(B):
                        v.wait_ge(S("rstd"), B * c + b + 1)
                        for q in range(NQ):
                            ins = v.tensor_scalar(n_tile[b][:, q, :], xm[b][:, q, :], mv[b][:, q, 0:1],
                                                  rs[b][:, q:q + 1], ALU.subtract, ALU.mult)
                        ins.then_inc(S("norm"), 1)
                    if not last:
                        scale(c + 1)
                    for b in range(B):
                        v.wait_ge(S("logits"), B * c + b + 1)
                        v.tensor_copy(lg[:, bass.ds(NQ * c + TB * b, NQ), :], psl[b])

                scale(0)
                with v.Fori(0, NC - 1) as c:
                    chunk(c, False)
                chunk(NC - 1, True)

                def wide(t):
                    return t.unsqueeze(2).to_broadcast([P, N, E_])

                def rows(t):
                    return t.unsqueeze(1).to_broadcast([P, N, E_])

                v.drain()
                v.tensor_reduce(c1[:], lg[:], AX.X, ALU.max)
                v.drain()
                v.tensor_tensor(lg[:], lg[:], wide(c1[:]), ALU.subtract).then_inc(S("shifted"), 1)
                v.wait_ge(S("exp"), 1)
                v.tensor_reduce(c1[:], lg[:], AX.X, ALU.add)
                v.drain()
                v.reciprocal(c1[:], c1[:])
                v.drain()
                v.tensor_tensor(lg[:], lg[:], wide(c1[:]), ALU.mult)
                v.drain()
                for n in range(N):
                    v.max(t8[:, n, :], lg[:, n, :])
                v.drain()
                for n in range(N):
                    v.max_index(i8[:, n, :], t8[:, n, :], lg[:, n, :])
                v.tensor_tensor(c1[:], t8[:, :, 0], t8[:, :, 1], ALU.add)
                v.drain()
                v.reciprocal(c1[:], c1[:])
                v.tensor_copy(fi[:], i8[:])
                v.drain()
                for k in range(2):
                    v.tensor_tensor(wts[:, :, k], t8[:, :, k], c1[:], ALU.mult)
                    v.tensor_tensor(m12[:, k], rows(iota[:, 0:E_]), wide(fi[:, :, k]), ALU.is_equal)
                v.drain()
                v.tensor_tensor(cnt[:], m12[:, 0], m12[:, 1], ALU.add).then_inc(S("count"), 1)
                v.wait_ge(S("prefix"), 1)
                v.tensor_copy(tot[:], psc[:, 1])
                v.drain()
                for e in range(E_):
                    v.tensor_tensor_scan(cum[:, :, e], tot[:, :, e], zero[:], 0.0, ALU.add, ALU.add)
                v.drain()
                v.tensor_scalar(tl[:, 0, :], iota[:, 0:N], float(P), None, ALU.mult)
                v.drain()
                v.tensor_copy(c1[:], tl[:, 0, :])
                v.drain()
                v.tensor_tensor(tl[:], cum[:, N - 1, :].unsqueeze(2).to_broadcast([P, E_, N]),
                                c1[:].unsqueeze(1).to_broadcast([P, E_, N]), ALU.is_gt)
                v.drain()
                v.tensor_reduce(te[:], tl[:], AX.X, ALU.add)
                v.drain()
                v.tensor_tensor_scan(tc[:], te[:], zero[:, 0:E_], 0.0, ALU.add, ALU.add)
                v.drain()
                v.tensor_tensor(off[:], tc[:], te[:], ALU.subtract)
                v.tensor_tensor(cum[:], cum[:], tot[:], ALU.subtract)
                v.drain()
                v.tensor_scalar(off[:], off[:], float(P), None, ALU.mult)
                v.tensor_tensor(cum[:], cum[:], psc[:, 0], ALU.add)
                v.drain()
                v.tensor_tensor(cum[:], cum[:], rows(off[:]), ALU.add)
                for k in range(2):
                    v.drain()
                    v.tensor_tensor(tmp[:], cum[:], m12[:, k], ALU.mult)
                    v.drain()
                    v.tensor_reduce(sf[:], tmp[:], AX.X, ALU.add)
                    v.drain()
                    v.tensor_copy(slot[:, :, k], sf[:])
                v.tensor_tensor(ee[:], iota[:].unsqueeze(2).to_broadcast([P, NT, E_ - 1]),
                                tc[:, 0:E_ - 1].unsqueeze(1).to_broadcast([P, NT, E_ - 1]), ALU.is_ge)
                v.drain()
                v.tensor_reduce(ef[:], ee[:], AX.X, ALU.add)
                v.drain()
                v.tensor_copy(eid[:], ef[:])


def expert_phase(nc, vec, ew, scr, eid, space):
    w1, w2, b1, b2 = ew
    with ExitStack() as ctx:
        used = [0]

        def cut(*shape):
            n = int(np.prod(shape))
            used[0] += n
            t = space[:, used[0] - n:used[0]]
            return t if len(shape) == 1 else t.rearrange("p (a b) -> p a b", b=shape[1])

        s = {}

        def S(name):
            if name not in s:
                s[name] = nc.alloc_semaphore(f"e_{name}")
            return s[name]

        FT = F // P
        ident = cut(P)
        xs = cut(C)
        xT = cut(CH, P)
        pre = cut(F)
        g = cut(F)
        hT = cut(FT, P)
        y = cut(C)
        psU = ctx.enter_context(nc.psum_tensor(f"e_up", [P, F], F32))
        psH = ctx.enter_context(nc.psum_tensor(f"e_ht", [P, FT, P], F32))
        psX = ctx.enter_context(nc.psum_tensor(f"e_xt", [P, CH, P], F32))
        psD = ctx.enter_context(nc.psum_tensor(f"e_down", [P, C], F32))
        xin = scr["x_slots"].rearrange("(j p) d -> j p d", p=P)
        yout = scr["y_slots"].rearrange("(j p) d -> j p d", p=P)
        L = NT - 1

        def expert(eng, j):
            return eng.value_load(eid[0:1, j:j + 1] if isinstance(j, int) else eid[0:1, bass.ds(j, 1)],
                                  min_val=0, max_val=E_ - 1)

        with nc.Block() as block:
            @block.sync
            def _(sp):
                def load(j):
                    wait(sp, S("x_turned"), j)
                    sp.dma_start(xs[:], xin[j]).then_inc(S("x_slots"), 16)

                load(0)
                with sp.Fori(1, NT) as j:
                    load(j)

            @block.gpsimd
            def _(pool):
                pool.memset(ident[:], 0.0)
                pool.drain()
                pool.affine_select(out=ident[:], in_=ident[:], compare_op=ALU.not_equal, fill=1.0, base=0,
                                   pattern=[[-1, P]], channel_multiplier=1)
                pool.drain()
                pool.nop().then_inc(S("consts"), 1)
                with pool.Fori(0, NT) as j:
                    pool.wait_ge(S("y"), j + 1)
                    pool.dma_start(yout[j], y[:]).then_inc(S("y_stored"), 16)
                pool.wait_ge(S("y_stored"), 16 * NT)

            @block.tensor
            def _(pe):
                def turn_x(j):
                    pe.wait_ge(S("x_slots"), 16 * j + 16)
                    wait(pe, S("xT"), j)
                    for d in range(CH):
                        ins = pe.transpose(psX[:, d, :], xs[:, d * P:(d + 1) * P], ident[:])
                    ins.then_inc(S("x_turned"), 1)

                def up(j, e):
                    pe.wait_ge(S("xT"), j + 1)
                    wait(pe, S("biased"), j)
                    for h in range(F // 512):
                        for d in range(CH):
                            ins = pe.matmul(psU[:, h * 512:(h + 1) * 512], xT[:, d, :],
                                            w1[:, d, e, h * 512:(h + 1) * 512], start=(d == 0), stop=(d == CH - 1))
                    ins.then_inc(S("up"), 1)

                def turn_h(j):
                    pe.wait_ge(S("gelu"), j + 1)
                    for f in range(FT):
                        if f % 4 == 0:
                            wait(pe, S(f"hT{f // 4}"), j)
                        ins = pe.transpose(psH[:, f, :], g[:, f * P:(f + 1) * P], ident[:])
                        if f % 4 == 3:
                            ins.then_inc(S("h_turned"), 1)

                def down(j, e):
                    wait(pe, S("y"), j)
                    for f in range(FT):
                        if f % 4 == 0:
                            pe.wait_ge(S(f"hT{f // 4}"), j + 1)
                        ins = pe.matmul(psD[:], hT[:, f, :], w2[:, f, e, :], start=(f == 0), stop=(f == FT - 1))
                    ins.then_inc(S("down"), 1)

                pe.wait_ge(S("consts"), 1)
                turn_x(0)
                up(0, expert(pe, 0))
                turn_x(1)
                turn_h(0)

                def step(j):
                    e, before = expert(pe, j), expert(pe, j - 1)
                    up(j, e)
                    turn_x(j + 1)
                    down(j - 1, before)
                    turn_h(j)

                step(1)
                with pe.Fori(2, NT - 1) as j:
                    step(j)
                up(L, expert(pe, L))
                down(L - 1, expert(pe, L - 1))
                turn_h(L)
                down(L, expert(pe, L))

            @block.scalar
            def _(act):
                def x_t(j):
                    act.wait_ge(S("x_turned"), j + 1)
                    wait(act, S("up"), j)
                    for d in range(CH):
                        ins = act.activation(xT[:, d, :], psX[:, d, :], ACT.Identity,
                                             scale=vec[:, VEC.index("ffn_ln2_g"), d:d + 1],
                                             bias=vec[:, VEC.index("ffn_ln2_b"), d:d + 1])
                    ins.then_inc(S("xT"), 1)

                def gelu(j):
                    act.wait_ge(S("biased"), j + 1)
                    act.activation(g[:], pre[:], ACT.Gelu_apprx_tanh).then_inc(S("gelu"), 1)

                def h_t(j):
                    act.wait_ge(S("h_turned"), 2 * j + 2)
                    act.copy(hT[:, FT // 2:, :], psH[:, FT // 2:, :]).then_inc(S("hT1"), 1)

                x_t(0)
                x_t(1)
                gelu(0)
                h_t(0)
                with act.Fori(1, NT - 1) as j:
                    x_t(j + 1)
                    gelu(j)
                    h_t(j)
                gelu(L)
                h_t(L)

            @block.vector
            def _(v):
                def bias(j):
                    e = expert(v, j)
                    wait(v, S("gelu"), j)
                    v.wait_ge(S("up"), j + 1)
                    v.tensor_tensor(pre[:], psU[:], b1[:, e, :], ALU.add).then_inc(S("biased"), 1)

                def h_t(j):
                    v.wait_ge(S("h_turned"), 2 * j + 1)
                    v.tensor_copy(hT[:, 0:FT // 2, :], psH[:, 0:FT // 2, :]).then_inc(S("hT0"), 1)

                def out(j):
                    e = expert(v, j)
                    wait(v, S("y_stored"), 16 * j)
                    v.wait_ge(S("down"), j + 1)
                    v.tensor_tensor(y[:], psD[:], b2[:, e, :], ALU.add).then_inc(S("y"), 1)

                bias(0)
                h_t(0)

                def step(j):
                    bias(j)
                    out(j - 1)
                    h_t(j)

                step(1)
                with v.Fori(2, NT) as j:
                    step(j)
                out(L)


def scatter_phase(nc, w, xn, slot, scr, w2):
    scattered = nc.alloc_semaphore("scattered")
    loaded = nc.alloc_semaphore("w2_loaded")
    with nc.Block() as block:
        @block.sync
        def _(sp):
            for e in range(E_):
                sp.dma_start(w2[:, :, e, :], w["W2"][e].rearrange("(k p) n -> p k n", p=P)).then_inc(loaded, 16)
            sp.wait_ge(loaded, 16 * E_)

        @block.gpsimd
        def _(pool):
            for n in range(N):
                for k in range(2):
                    pool.indirect_dma_start(scr["x_slots"], bass.IndirectOffsetOnAxis(ap=slot[:, n, k:k + 1], axis=0),
                                            xn[:, n, :], None).then_inc(scattered, 16)
            pool.wait_ge(scattered, 16 * 2 * N)


def combine_phase(nc, scr, slot, wts, out):
    with ExitStack() as ctx:
        def sb(name, shape, dt=F32):
            return ctx.enter_context(nc.sbuf_tensor("c_" + name, shape, dt))

        s = {}

        def S(name):
            if name not in s:
                s[name] = nc.alloc_semaphore("c_" + name)
            return s[name]

        NS = N // NQ
        ye, xm, xo = ([sb(f"{n}{k}", [P, m, C]) for k in range(2)]
                      for n, m in (("y", 2 * NQ), ("x_mid", NQ), ("x_outer", NQ)))
        st = sb("stats", [P, NQ, 6])
        mv = sb("mean_var", [P, NQ, 2])
        rs = sb("rstd", [P, NQ])
        mhalf = sb("minus_half", [P, NQ])

        def steps_of(t):
            return t.rearrange("b (n q p) d -> (b n) p q d", p=P, q=NQ)

        xin, oin, dst = steps_of(scr["x_mid"]), steps_of(scr["X1"]), steps_of(out)

        with nc.Block() as block:
            @block.sync
            def _(sp):
                def load(n):
                    sp.dma_start(xm[n % 2][:], xin[n]).then_inc(S(f"loaded{n % 2}"), 16)
                    sp.dma_start(xo[n % 2][:], oin[n]).then_inc(S(f"loaded{n % 2}"), 16)

                load(0)
                load(1)
                for n in range(NS):
                    sp.wait_ge(S("done"), n + 1)
                    sp.dma_start(dst[n], xo[n % 2][:]).then_inc(S(f"stored{n % 2}"), 16)
                    if n + 2 < NS:
                        sp.wait_ge(S(f"stored{n % 2}"), 16 * (n // 2) + 16)
                        load(n + 2)
                for k in range(2):
                    sp.wait_ge(S(f"stored{k}"), 16 * NS // 2)

            @block.gpsimd
            def _(pool):
                pool.memset(mhalf[:], -0.5)
                pool.drain()

                def gather(n):
                    wait(pool, S("summed"), n - 1)
                    for j in range(2 * NQ):
                        pool.indirect_dma_start(ye[n % 2][:, j, :], None, scr["y_slots"], bass.IndirectOffsetOnAxis(
                            ap=slot[:, NQ * n + j // 2, j % 2:j % 2 + 1], axis=0)).then_inc(
                            S(f"gathered{n % 2}"), 16)

                def rstd(n):
                    pool.wait_ge(S("stats"), n + 1)
                    pool.tensor_tensor(rs[:], rs[:], mhalf[:], ALU.pow).then_inc(S("rstd"), 1)

                gather(0)
                gather(1)
                for n in range(NS):
                    rstd(n)
                    if n + 2 < NS:
                        gather(n + 2)

            @block.vector
            def _(v):
                for n in range(NS):
                    k = n % 2
                    y, xk = ye[k], xm[k]
                    v.wait_ge(S(f"loaded{k}"), 32 * (n // 2) + 32)
                    v.wait_ge(S(f"gathered{k}"), 16 * 2 * NQ * (n // 2) + 16 * 2 * NQ)
                    for j in range(2):
                        for q in range(NQ):
                            ins = v.scalar_tensor_tensor(xk[:, q, :], y[:, 2 * q + j, :],
                                                         wts[:, NQ * n + q, j:j + 1], xk[:, q, :], ALU.mult, ALU.add)
                        if j == 1:
                            ins.then_inc(S("summed"), 1)
                        v.drain()
                    for q in range(NQ):
                        v.bn_stats(st[:, q, :], xk[:, q, :])
                    v.drain()
                    for q in range(NQ):
                        v.bn_aggr(mv[:, q, :], st[:, q, :])
                    v.drain()
                    v.tensor_scalar(rs[:], mv[:, :, 1], EPS, None, ALU.add).then_inc(S("stats"), 1)
                    v.wait_ge(S("rstd"), n + 1)
                    for q in range(NQ):
                        v.tensor_scalar(xk[:, q, :], xk[:, q, :], mv[:, q, 0:1], rs[:, q:q + 1], ALU.subtract,
                                        ALU.mult)
                    v.drain()
                    v.tensor_tensor(xo[k][:], xo[k][:], xk[:], ALU.add).then_inc(S("done"), 1)


class ExpertLoads:

    def __init__(self, nc, ctx, w, vecs, scr):
        def sb(name, shape):
            return ctx.enter_context(nc.sbuf_tensor("expert_" + name, shape, F32))

        self.w, self.vecs, self.scr = w, vecs, scr
        self.vec = sb("vec", [P, len(VEC), CH])
        self.w1 = sb("w1", [P, CH, E_, F])
        self.b1 = sb("b1", [P, E_, F])
        self.b2 = sb("b2", [P, E_, C])
        self.zero = sb("zero_row", [P, C])
        self.loaded = nc.alloc_semaphore("experts_loaded")

    def clear(self, pool):
        pool.memset(self.zero[:], 0.0)

    def start(self, sp):
        sp.dma_start(self.vec[:], self.vecs).then_inc(self.loaded, 16)
        for e in range(E_):
            sp.dma_start(self.w1[:, :, e, :], self.w["W1"][e].rearrange("(k p) n -> p k n", p=P)).then_inc(
                self.loaded, 16)
        sp.dma_start(self.b1[:], self.w["b1"].partition_broadcast(P)).then_inc(self.loaded, 16)
        sp.dma_start(self.b2[:], self.w["b2"].partition_broadcast(P)).then_inc(self.loaded, 16)
        sp.dma_start(self.scr["x_slots"].rearrange("(p t) d -> p t d", p=P),
                     self.zero[:].unsqueeze(1).to_broadcast([P, NT, C])).then_inc(self.loaded, 16)

    def finish(self, sp):
        sp.wait_ge(self.loaded, 16 * (E_ + 4))


def moe_layer(nc, w, pre, scr, out):
    with ExitStack() as ctx:
        def sb(name, shape, dt=F32):
            return ctx.enter_context(nc.sbuf_tensor(name, shape, dt))

        slot = sb("slot", [P, N, 2], I32)
        wts = sb("weights", [P, N, 2])
        eid = sb("eid", [P, NT], I32)
        with ExitStack() as inner:
            xn = inner.enter_context(nc.sbuf_tensor("xn", [P, N, C], F32))
            route_phase(nc, w, pre.vec, scr, xn, slot, wts, eid)
            w2 = inner.enter_context(nc.sbuf_tensor("expert_w2", [P, F // P, E_, C], F32))
            scatter_phase(nc, w, xn, slot, scr, w2)
            expert_phase(nc, pre.vec, (pre.w1, w2, pre.b1, pre.b2), scr, eid,
                         xn[:].rearrange("p n c -> p (n c)"))
        combine_phase(nc, scr, slot, wts, out)


INPUTS = {
    "x": "L0_attn_x",
    **{n: "L0_attn_" + n for n in ("att_Wk", "att_Wv", "att_Wr", "att_Wo", "ffn_Wk", "ffn_Wr", "ffn_Wv")},
    **{n: "L0_ffn_" + n for n in ("Wq", "Wk", "Wv", "Wo", "Wg", "W1", "b1", "W2", "b2")},
}
ATTN_VEC = {n: "L0_attn_" + n for n in ("time_decay", "time_first", "time_mix_k", "time_mix_v", "time_mix_r", "cm_k",
                                        "cm_r")}
ATTN_VEC.update({f"attn_ln{k}_{c}": f"L0_attn_ln{k}_{c}" for k in (1, 2) for c in "gb"})
ATTN_VEC.update({f"ffn_ln{k}_{c}": f"L0_ffn_ln{k}_{c}" for k in (1, 2) for c in "gb"})


def sandwich(nc, w, out):
    def scratch(name, shape, dt=F32):
        return nc.dram_tensor("scr_" + name, shape, dt, kind="Internal").ap()

    scr = {
        "X1": scratch("X1", (B, T, C)),
        "h1": scratch("h1", (B, T, C)),
        "v_aug": scratch("v_aug", (B, T // P, P, HEADS * 2 * DH)),
        "parts": scratch("parts", (2, NPART, C, B, T), BF16),
        "ctx": scratch("ctx", (NWIN, P, QW)),
        "inv": scratch("inv", (NWIN * 4, QW)),
        "x_mid": scratch("x_mid", (B, T, C)),
        "x_slots": scratch("x_slots", (NT * P, C)),
        "y_slots": scratch("y_slots", (NT * P, C)),
    }
    rwkv_phase(nc, w["x"], w["vecs"], w, scr)
    with ExitStack() as ctx:
        expert_loads = ExpertLoads(nc, ctx, w, w["vecs"], scr)
        attention_phase(nc, scr, expert_loads)
        moe_layer(nc, w, expert_loads, scr, out)


def kernel(**inputs):
    import numpy as np
    import concourse.bacc as bacc
    from concourse.bass_utils import run_bass_kernel_spmd

    arrays = {n: np.ascontiguousarray(inputs[k]) for n, k in INPUTS.items()}
    for n in ("att_Wk", "att_Wv", "att_Wr", "att_Wo", "ffn_Wk", "ffn_Wr", "ffn_Wv"):
        arrays[n] = np.ascontiguousarray(np.asarray(inputs[INPUTS[n]]).T)
    vecs = np.stack([np.asarray(inputs[ATTN_VEC[n]]) for n in VEC])
    arrays["vecs"] = np.ascontiguousarray(vecs.reshape(len(VEC), CH, P).transpose(2, 0, 1))
    nc = bacc.Bacc("TRN2", target_bir_lowering=False, num_devices=1)
    w = {n: nc.dram_tensor(f"in_{n}", a.shape, mybir.dt.from_np(a.dtype), kind="ExternalInput").ap()
         for n, a in arrays.items()}
    out = nc.dram_tensor("out_x", (B, T, C), F32, kind="ExternalOutput").ap()
    sandwich(nc, w, out)
    r = run_bass_kernel_spmd(nc, [{f"in_{n}": a for n, a in arrays.items()}], core_ids=[0])
    return r.results[0]["out_x"]
```
